# Optimizing a Trainium2 kernel written in Bass

```python
import numpy as np
import jax
import jax.numpy as jnp

def _softmax(x, axis=-1):
    return jax.nn.softmax(x, axis=axis)

def _gelu(x):
    return jax.nn.gelu(x, approximate=True)

def _silu(x):
    return jax.nn.silu(x)

def _sigmoid(x):
    return jax.nn.sigmoid(x)

def _layernorm(x, axis=-1, eps=1e-05):
    m = jnp.mean(x, axis=axis, keepdims=True)
    v = jnp.var(x, axis=axis, keepdims=True)
    return (x - m) / jnp.sqrt(v + eps)

def _scatter_add(tgt, idx, src, axis=0):
    return tgt.at[idx].add(src)

def _segment_sum(src, seg, n):
    return jax.ops.segment_sum(src, seg, n)
kernel_name = 'mk_rec_standalone_d1_rec_r8_fffba0'

def setup_inputs(seed: int=0):
    np.random.seed(seed)
    _w = jnp.asarray

    def _rec_inputs():
        import jax
        import jax.numpy as jnp
        _rk = jax.random.key(seed)
        r_items = jnp.stack([jax.random.randint(jax.random.fold_in(jax.random.fold_in(_rk, 1), 0), (1024,), 76, 99919, jnp.int32), jax.random.randint(jax.random.fold_in(jax.random.fold_in(_rk, 1), 1), (1024,), 55, 99454, jnp.int32), jax.random.randint(jax.random.fold_in(jax.random.fold_in(_rk, 1), 2), (1024,), 29, 99986, jnp.int32), jax.random.randint(jax.random.fold_in(jax.random.fold_in(_rk, 1), 3), (1024,), 67, 99935, jnp.int32), jax.random.randint(jax.random.fold_in(jax.random.fold_in(_rk, 1), 4), (1024,), 209, 99887, jnp.int32), jax.random.randint(jax.random.fold_in(jax.random.fold_in(_rk, 1), 5), (1024,), 176, 99942, jnp.int32), jax.random.randint(jax.random.fold_in(jax.random.fold_in(_rk, 1), 6), (1024,), 1, 99939, jnp.int32), jax.random.randint(jax.random.fold_in(jax.random.fold_in(_rk, 1), 7), (1024,), 31, 99945, jnp.int32), jax.random.randint(jax.random.fold_in(jax.random.fold_in(_rk, 1), 8), (1024,), 95, 99951, jnp.int32), jax.random.randint(jax.random.fold_in(jax.random.fold_in(_rk, 1), 9), (1024,), 13, 12482, jnp.int32), jax.random.randint(jax.random.fold_in(jax.random.fold_in(_rk, 1), 10), (1024,), 70, 99701, jnp.int32), jax.random.randint(jax.random.fold_in(jax.random.fold_in(_rk, 1), 11), (1024,), 146, 99964, jnp.int32), jax.random.randint(jax.random.fold_in(jax.random.fold_in(_rk, 1), 12), (1024,), 39, 12467, jnp.int32), jax.random.randint(jax.random.fold_in(jax.random.fold_in(_rk, 1), 13), (1024,), 6, 99887, jnp.int32), jax.random.randint(jax.random.fold_in(jax.random.fold_in(_rk, 1), 14), (1024,), 323, 99835, jnp.int32), jax.random.randint(jax.random.fold_in(jax.random.fold_in(_rk, 1), 15), (1024,), 131, 99917, jnp.int32), jax.random.randint(jax.random.fold_in(jax.random.fold_in(_rk, 1), 16), (1024,), 28, 99865, jnp.int32), jax.random.randint(jax.random.fold_in(jax.random.fold_in(_rk, 1), 17), (1024,), 20, 99962, jnp.int32), jax.random.randint(jax.random.fold_in(jax.random.fold_in(_rk, 1), 18), (1024,), 86, 99873, jnp.int32), jax.random.randint(jax.random.fold_in(jax.random.fold_in(_rk, 1), 19), (1024,), 18, 12488, jnp.int32), jax.random.randint(jax.random.fold_in(jax.random.fold_in(_rk, 1), 20), (1024,), 17, 99987, jnp.int32), jax.random.randint(jax.random.fold_in(jax.random.fold_in(_rk, 1), 21), (1024,), 231, 99946, jnp.int32), jax.random.randint(jax.random.fold_in(jax.random.fold_in(_rk, 1), 22), (1024,), 264, 99913, jnp.int32), jax.random.randint(jax.random.fold_in(jax.random.fold_in(_rk, 1), 23), (1024,), 32, 99861, jnp.int32), jax.random.randint(jax.random.fold_in(jax.random.fold_in(_rk, 1), 24), (1024,), 78, 99953, jnp.int32), jax.random.randint(jax.random.fold_in(jax.random.fold_in(_rk, 1), 25), (1024,), 90, 12459, jnp.int32), jax.random.randint(jax.random.fold_in(jax.random.fold_in(_rk, 1), 26), (1024,), 98, 99911, jnp.int32), jax.random.randint(jax.random.fold_in(jax.random.fold_in(_rk, 1), 27), (1024,), 104, 99805, jnp.int32), jax.random.randint(jax.random.fold_in(jax.random.fold_in(_rk, 1), 28), (1024,), 71, 99870, jnp.int32), jax.random.randint(jax.random.fold_in(jax.random.fold_in(_rk, 1), 29), (1024,), 185, 99594, jnp.int32), jax.random.randint(jax.random.fold_in(jax.random.fold_in(_rk, 1), 30), (1024,), 394, 99938, jnp.int32), jax.random.randint(jax.random.fold_in(jax.random.fold_in(_rk, 1), 31), (1024,), 116, 99794, jnp.int32), jax.random.randint(jax.random.fold_in(jax.random.fold_in(_rk, 1), 32), (1024,), 100, 99954, jnp.int32), jax.random.randint(jax.random.fold_in(jax.random.fold_in(_rk, 1), 33), (1024,), 17, 99946, jnp.int32), jax.random.randint(jax.random.fold_in(jax.random.fold_in(_rk, 1), 34), (1024,), 46, 99945, jnp.int32), jax.random.randint(jax.random.fold_in(jax.random.fold_in(_rk, 1), 35), (1024,), 19, 99949, jnp.int32), jax.random.randint(jax.random.fold_in(jax.random.fold_in(_rk, 1), 36), (1024,), 148, 99807, jnp.int32), jax.random.randint(jax.random.fold_in(jax.random.fold_in(_rk, 1), 37), (1024,), 64, 99906, jnp.int32), jax.random.randint(jax.random.fold_in(jax.random.fold_in(_rk, 1), 38), (1024,), 53, 99948, jnp.int32), jax.random.randint(jax.random.fold_in(jax.random.fold_in(_rk, 1), 39), (1024,), 14, 99978, jnp.int32), jax.random.randint(jax.random.fold_in(jax.random.fold_in(_rk, 1), 40), (1024,), 88, 99969, jnp.int32), jax.random.randint(jax.random.fold_in(jax.random.fold_in(_rk, 1), 41), (1024,), 1, 99884, jnp.int32), jax.random.randint(jax.random.fold_in(jax.random.fold_in(_rk, 1), 42), (1024,), 79, 99847, jnp.int32), jax.random.randint(jax.random.fold_in(jax.random.fold_in(_rk, 1), 43), (1024,), 45, 99942, jnp.int32), jax.random.randint(jax.random.fold_in(jax.random.fold_in(_rk, 1), 44), (1024,), 5, 12484, jnp.int32), jax.random.randint(jax.random.fold_in(jax.random.fold_in(_rk, 1), 45), (1024,), 213, 99855, jnp.int32), jax.random.randint(jax.random.fold_in(jax.random.fold_in(_rk, 1), 46), (1024,), 142, 99809, jnp.int32), jax.random.randint(jax.random.fold_in(jax.random.fold_in(_rk, 1), 47), (1024,), 62, 99821, jnp.int32), jax.random.randint(jax.random.fold_in(jax.random.fold_in(_rk, 1), 48), (1024,), 3, 99964, jnp.int32), jax.random.randint(jax.random.fold_in(jax.random.fold_in(_rk, 1), 49), (1024,), 82, 99919, jnp.int32)], axis=1)
        r_inputs = jnp.stack([jax.random.randint(jax.random.fold_in(jax.random.fold_in(_rk, 2), 0), (1024,), 55, 99965, jnp.int32), jax.random.randint(jax.random.fold_in(jax.random.fold_in(_rk, 2), 1), (1024,), 48, 12493, jnp.int32), jax.random.randint(jax.random.fold_in(jax.random.fold_in(_rk, 2), 2), (1024,), 149, 99818, jnp.int32), jax.random.randint(jax.random.fold_in(jax.random.fold_in(_rk, 2), 3), (1024,), 64, 99943, jnp.int32), jax.random.randint(jax.random.fold_in(jax.random.fold_in(_rk, 2), 4), (1024,), 83, 99948, jnp.int32), jax.random.randint(jax.random.fold_in(jax.random.fold_in(_rk, 2), 5), (1024,), 54, 99999, jnp.int32), jax.random.randint(jax.random.fold_in(jax.random.fold_in(_rk, 2), 6), (1024,), 215, 99939, jnp.int32), jax.random.randint(jax.random.fold_in(jax.random.fold_in(_rk, 2), 7), (1024,), 95, 99911, jnp.int32), jax.random.randint(jax.random.fold_in(jax.random.fold_in(_rk, 2), 8), (1024,), 33, 99809, jnp.int32), jax.random.randint(jax.random.fold_in(jax.random.fold_in(_rk, 2), 9), (1024,), 67, 99845, jnp.int32), jax.random.randint(jax.random.fold_in(jax.random.fold_in(_rk, 2), 10), (1024,), 35, 99948, jnp.int32), jax.random.randint(jax.random.fold_in(jax.random.fold_in(_rk, 2), 11), (1024,), 56, 99973, jnp.int32), jax.random.randint(jax.random.fold_in(jax.random.fold_in(_rk, 2), 12), (1024,), 30, 99941, jnp.int32), jax.random.randint(jax.random.fold_in(jax.random.fold_in(_rk, 2), 13), (1024,), 97, 99859, jnp.int32), jax.random.randint(jax.random.fold_in(jax.random.fold_in(_rk, 2), 14), (1024,), 23, 99998, jnp.int32), jax.random.randint(jax.random.fold_in(jax.random.fold_in(_rk, 2), 15), (1024,), 116, 99994, jnp.int32), jax.random.randint(jax.random.fold_in(jax.random.fold_in(_rk, 2), 16), (1024,), 148, 12495, jnp.int32), jax.random.randint(jax.random.fold_in(jax.random.fold_in(_rk, 2), 17), (1024,), 206, 99747, jnp.int32), jax.random.randint(jax.random.fold_in(jax.random.fold_in(_rk, 2), 18), (1024,), 37, 99628, jnp.int32), jax.random.randint(jax.random.fold_in(jax.random.fold_in(_rk, 2), 19), (1024,), 324, 12483, jnp.int32), jax.random.randint(jax.random.fold_in(jax.random.fold_in(_rk, 2), 20), (1024,), 89, 12495, jnp.int32), jax.random.randint(jax.random.fold_in(jax.random.fold_in(_rk, 2), 21), (1024,), 68, 99881, jnp.int32), jax.random.randint(jax.random.fold_in(jax.random.fold_in(_rk, 2), 22), (1024,), 2, 99711, jnp.int32), jax.random.randint(jax.random.fold_in(jax.random.fold_in(_rk, 2), 23), (1024,), 311, 99742, jnp.int32), jax.random.randint(jax.random.fold_in(jax.random.fold_in(_rk, 2), 24), (1024,), 53, 99950, jnp.int32), jax.random.randint(jax.random.fold_in(jax.random.fold_in(_rk, 2), 25), (1024,), 190, 99982, jnp.int32), jax.random.randint(jax.random.fold_in(jax.random.fold_in(_rk, 2), 26), (1024,), 216, 99910, jnp.int32), jax.random.randint(jax.random.fold_in(jax.random.fold_in(_rk, 2), 27), (1024,), 148, 99953, jnp.int32), jax.random.randint(jax.random.fold_in(jax.random.fold_in(_rk, 2), 28), (1024,), 137, 99935, jnp.int32), jax.random.randint(jax.random.fold_in(jax.random.fold_in(_rk, 2), 29), (1024,), 122, 12485, jnp.int32), jax.random.randint(jax.random.fold_in(jax.random.fold_in(_rk, 2), 30), (1024,), 8, 99927, jnp.int32), jax.random.randint(jax.random.fold_in(jax.random.fold_in(_rk, 2), 31), (1024,), 13, 99979, jnp.int32), jax.random.randint(jax.random.fold_in(jax.random.fold_in(_rk, 2), 32), (1024,), 120, 99930, jnp.int32), jax.random.randint(jax.random.fold_in(jax.random.fold_in(_rk, 2), 33), (1024,), 49, 99972, jnp.int32), jax.random.randint(jax.random.fold_in(jax.random.fold_in(_rk, 2), 34), (1024,), 134, 99879, jnp.int32), jax.random.randint(jax.random.fold_in(jax.random.fold_in(_rk, 2), 35), (1024,), 12, 99958, jnp.int32), jax.random.randint(jax.random.fold_in(jax.random.fold_in(_rk, 2), 36), (1024,), 168, 12497, jnp.int32), jax.random.randint(jax.random.fold_in(jax.random.fold_in(_rk, 2), 37), (1024,), 57, 99894, jnp.int32), jax.random.randint(jax.random.fold_in(jax.random.fold_in(_rk, 2), 38), (1024,), 231, 99987, jnp.int32), jax.random.randint(jax.random.fold_in(jax.random.fold_in(_rk, 2), 39), (1024,), 35, 99956, jnp.int32), jax.random.randint(jax.random.fold_in(jax.random.fold_in(_rk, 2), 40), (1024,), 23, 12490, jnp.int32), jax.random.randint(jax.random.fold_in(jax.random.fold_in(_rk, 2), 41), (1024,), 114, 99951, jnp.int32), jax.random.randint(jax.random.fold_in(jax.random.fold_in(_rk, 2), 42), (1024,), 0, 99894, jnp.int32), jax.random.randint(jax.random.fold_in(jax.random.fold_in(_rk, 2), 43), (1024,), 158, 99699, jnp.int32), jax.random.randint(jax.random.fold_in(jax.random.fold_in(_rk, 2), 44), (1024,), 28, 99839, jnp.int32), jax.random.randint(jax.random.fold_in(jax.random.fold_in(_rk, 2), 45), (1024,), 5, 99956, jnp.int32), jax.random.randint(jax.random.fold_in(jax.random.fold_in(_rk, 2), 46), (1024,), 69, 99986, jnp.int32), jax.random.randint(jax.random.fold_in(jax.random.fold_in(_rk, 2), 47), (1024,), 4, 99981, jnp.int32), jax.random.randint(jax.random.fold_in(jax.random.fold_in(_rk, 2), 48), (1024,), 55, 99931, jnp.int32), jax.random.randint(jax.random.fold_in(jax.random.fold_in(_rk, 2), 49), (1024,), 82, 99978, jnp.int32)], axis=1)
        r_alias_inputs = jax.random.randint(jax.random.fold_in(_rk, 3), (1024, 50), 0, 50, jnp.int32)
        return (r_items, r_inputs, r_alias_inputs)
    r_items, r_inputs, r_alias_inputs = _rec_inputs()

    def _L0_rec_setup():
        import jax, jax.numpy as jnp
        import numpy as np
        N = 12500
        D = 128
        B = 1024
        L = 50
        NNZ = 200000
        LAYERS = 2
        W_K = 12.0
        EPS = 1e-12

        def _l2norm(x):
            n = jnp.sqrt(jnp.sum(x * x, axis=-1, keepdims=True))
            return x / jnp.maximum(n, EPS)
        key = jax.random.key(seed)
        ks = jax.random.split(key, 12)
        stdv = 1.0 / np.sqrt(D)
        u = lambda k, shape: jax.random.uniform(k, shape, jnp.float32, -stdv, stdv)
        inp = {'items': jax.random.randint(ks[0], (B, L), 0, N), 'inputs': jax.random.randint(ks[1], (B, L), 0, N), 'alias_inputs': jax.random.randint(ks[2], (B, L), 0, L), 'adj_row': jnp.sort(jax.random.randint(ks[3], (NNZ,), 0, N)), 'adj_col': jax.random.randint(ks[4], (NNZ,), 0, N), 'adj_val': jax.random.uniform(ks[5], (NNZ,), jnp.float32), 'E': u(ks[6], (N, D)), 'pos_emb': u(ks[7], (L, D)), 'w1': u(ks[8], (2 * D, D)), 'w2': u(ks[9], (D, 1)), 'glu1_w': u(ks[10], (D, D)), 'glu1_b': jnp.zeros((D,), jnp.float32), 'glu2_w': u(ks[11], (D, D))}
        return inp
    _L0_rec_all = _L0_rec_setup()
    _L0_rec_in = {k: v for k, v in _L0_rec_all.items() if k in ('adj_row', 'adj_col', 'adj_val', 'E', 'pos_emb', 'w1', 'w2', 'glu1_w', 'glu1_b', 'glu2_w')}
    del _L0_rec_all
    return {'r_items': r_items, 'r_inputs': r_inputs, 'r_alias_inputs': r_alias_inputs, 'L0_rec_adj_row': _L0_rec_in['adj_row'], 'L0_rec_adj_col': _L0_rec_in['adj_col'], 'L0_rec_adj_val': _L0_rec_in['adj_val'], 'L0_rec_E': _L0_rec_in['E'], 'L0_rec_pos_emb': _L0_rec_in['pos_emb'], 'L0_rec_w1': _L0_rec_in['w1'], 'L0_rec_w2': _L0_rec_in['w2'], 'L0_rec_glu1_w': _L0_rec_in['glu1_w'], 'L0_rec_glu1_b': _L0_rec_in['glu1_b'], 'L0_rec_glu2_w': _L0_rec_in['glu2_w']}

def reference(r_items, r_inputs, r_alias_inputs, L0_rec_adj_row, L0_rec_adj_col, L0_rec_adj_val, L0_rec_E, L0_rec_pos_emb, L0_rec_w1, L0_rec_w2, L0_rec_glu1_w, L0_rec_glu1_b, L0_rec_glu2_w):
    import jax
    import jax.numpy as jnp

    def _L0_rec_ref(items, inputs, alias_inputs, adj_row, adj_col, adj_val, E, pos_emb, w1, w2, glu1_w, glu1_b, glu2_w):
        import jax, jax.numpy as jnp
        import numpy as np
        N = 12500
        D = 128
        B = 1024
        L = 50
        NNZ = 200000
        LAYERS = 2
        W_K = 12.0
        EPS = 1e-12

        def _l2norm(x):
            n = jnp.sqrt(jnp.sum(x * x, axis=-1, keepdims=True))
            return x / jnp.maximum(n, EPS)

        def spmm(h):
            return jax.ops.segment_sum(adj_val[:, None] * h[adj_col], adj_row, num_segments=N)
        h = E
        acc = E
        for _ in range(LAYERS):
            h = _l2norm(spmm(h))
            acc = acc + h
        graph_item_embs = acc / (LAYERS + 1)
        hidden = graph_item_embs[items]
        seq_hidden = jnp.take_along_axis(hidden, alias_inputs[..., None], axis=1)
        mask = (inputs != 0).astype(seq_hidden.dtype)[..., None]
        hs = jnp.sum(seq_hidden * mask, axis=1) / jnp.sum(mask, axis=1)
        pos = jnp.flip(pos_emb, axis=0)
        pos_b = jnp.broadcast_to(pos[None], (seq_hidden.shape[0], L, D))
        nh = jnp.tanh(jnp.concatenate([pos_b, seq_hidden], axis=-1) @ w1)
        nh = jax.nn.sigmoid(nh @ glu1_w.T + glu1_b + (hs @ glu2_w.T)[:, None, :])
        beta = nh @ w2 * mask
        sess_emb = jnp.sum(beta * seq_hidden, axis=1)
        select = W_K * _l2norm(sess_emb)
        scores = select @ _l2norm(graph_item_embs).T
        return scores
    y = _L0_rec_ref(r_items, r_inputs, r_alias_inputs, L0_rec_adj_row, L0_rec_adj_col, L0_rec_adj_val, L0_rec_E, L0_rec_pos_emb, L0_rec_w1, L0_rec_w2, L0_rec_glu1_w, L0_rec_glu1_b, L0_rec_glu2_w)
    return y

_drawn_inputs = setup_inputs


def setup_inputs(seed=0):
    import zlib

    import numpy as np

    out = dict(_drawn_inputs(seed))
    spreads = {'L0_rec_glu1_b': (0.0, 0.8)}
    factors = {'L0_rec_pos_emb': 8.0,
     'L0_rec_w1': 8.0,
     'L0_rec_w2': 5.12,
     'L0_rec_glu1_w': 6.648,
     'L0_rec_glu2_w': 27.07}
    for name, (base, spread) in spreads.items():
        noise = np.random.default_rng([zlib.crc32(name.encode()), seed]).standard_normal(out[name].shape)
        drawn = base * np.exp(spread * noise) if base else spread * noise
        out[name] = jnp.asarray(drawn.astype(out[name].dtype))
    for name, factor in factors.items():
        out[name] = (out[name] * factor).astype(out[name].dtype)
    return out
```

```python
from contextlib import ExitStack

import concourse.bass as bass
from concourse import mybir

ALU = mybir.AluOpType
ACT = mybir.ActivationFunctionType
AX_X = mybir.AxisListType.X
F32 = mybir.dt.float32
I32 = mybir.dt.int32

P = 128
LAYERS = 2
RING = 16
GROUP = 4
BODY = 32
SLOTS = 4
BLOCK = 256
HALVES = BLOCK // P
NOWHERE = 1 << 20
STAGES = 4
NC = 512
W_K = 12.0
EPS = 1e-12


def rec_kernel(nc, items, inputs, alias, adj_row, adj_col, adj_val, E, pos_emb, w1, w2, glu1_w, glu1_b, glu2_w, out):
    N, D = E.shape
    B, L = items.shape
    NNZ = adj_row.shape[0]
    FULL = NNZ // P
    REST = NNZ - FULL * P
    TILES = FULL + 1
    NB = -(-N // BLOCK)
    NJ = NB * HALVES
    NP = NB * BLOCK
    STEPS = -(-(TILES + NB - 1) // RING) * RING
    LAPS = STEPS // RING
    SC = -(-STEPS // P)
    LOOPS = NB
    TAIL = STEPS - LOOPS * BODY
    KB = B // P
    GS = [4] * (L // 4) + ([L % 4] if L % 4 else [])
    NG = len(GS)
    NCH = -(-N // NC)
    PAIRS = -(-NCH // 2)
    USES = [len(range(i, PAIRS, STAGES)) for i in range(STAGES)]
    C0 = 5
    SHARE = [0] * C0 + [NCH // (NG - C0) + (i < NCH % (NG - C0)) for i in range(NG - C0)]
    CHUNKS = [list(range(sum(SHARE[:g]), sum(SHARE[:g + 1]))) for g in range(NG)]
    assert 0 < REST < P and TAIL % GROUP == 0 and LOOPS * BODY + TAIL == STEPS and D == P

    nc.disable_value_cache = True
    edge_tiles = nc.dram_tensor("edge_tiles", (TILES + 1, 3, P), I32, kind="Internal").ap()
    h1_dram = nc.dram_tensor("h1_dram", (NP, D), F32, kind="Internal").ap()
    graph_dram = nc.dram_tensor("graph_dram", (NP, D), F32, kind="Internal").ap()

    with ExitStack() as ctx:
        def sb(name, shape, dt=F32):
            return ctx.enter_context(nc.sbuf_tensor(name, shape, dt))

        def sem(name):
            return ctx.enter_context(nc.semaphore(name))

        def pb(name, shape):
            return ctx.enter_context(nc.psum_tensor(name, shape, F32))

        sumA = sb("sumA", [P, NB, BLOCK])
        sumB = sb("sumB", [P, NB, BLOCK])
        seq = sb("seq", [P, 2, L, D])
        share1 = sb("share1", [P, STAGES * 2 * NC])
        ring = share1[:, 0:RING * D].rearrange("p (s d) -> p s d", d=D)
        onehot = share1[:, RING * D:RING * D + SLOTS * BLOCK].rearrange("p (s f) -> p s f", f=BLOCK)
        e_rows = share1[:, RING * D + SLOTS * BLOCK:RING * D + (SLOTS + 1) * BLOCK].rearrange("p (h d) -> p h d", d=D)
        stage = share1[:].rearrange("p (s f) -> p s f", s=STAGES)
        share2 = sb("share2", [P, max(2 * SC * P, 6 * NC)])
        rowT = share2[:, 0:SC * P]
        valT = share2[:, SC * P:2 * SC * P]
        xT = share2[:, 0:2 * NC].rearrange("p (s f) -> p s f", s=2)
        z = share2[:, 2 * NC:4 * NC].rearrange("p (s f) -> p s f", s=2)
        gate = share2[:, 4 * NC:6 * NC].rearrange("p (s f) -> p s f", s=2)
        colT = sb("colT", [P, SC * P], I32)
        block_of = sb("block_of", [1, SC * P], I32)
        cur = sb("cur", [P, RING], I32)
        ident = sb("ident", [P, P])
        iota_i = sb("iota_i", [P, BLOCK], I32)
        scol_i = sb("scol_i", [P, SC], I32)
        scol = sb("scol", [P, SC])
        tcol = sb("tcol", [P, SC])
        tcol_i = sb("tcol_i", [P, SC], I32)
        bcol = sb("bcol", [P, SC])
        b256 = sb("b256", [P, SC])
        ones = sb("ones", [1, P])
        pad = sb("pad", [2, 3, P], I32)
        ssq = sb("ssq", [P, NJ])
        nrm = sb("nrm", [P, NJ])
        inv = sb("inv", [P, NJ])
        cur_seq = sb("cur_seq", [P, 2, L], I32)
        rcnt = sb("rcnt", [P, KB])
        w1_sb = sb("w1_sb", [P, 2, D])
        w2_sb = sb("w2_sb", [P, 1])
        glu_sb = sb("glu_sb", [P, 2, D])
        gluT = sb("gluT", [P, 2, D])
        b1_sb = sb("b1_sb", [P, 1])
        pos_sb = sb("pos_sb", [L, D])
        posT = sb("posT", [P, L])
        posW = sb("posW", [P, L])
        hs = sb("hs", [P, D])
        hsT = sb("hsT", [P, P])
        hgT = sb("hgT", [P, P])
        beta = sb("beta", [P, L])
        sess = sb("sess", [P, D])
        sess_sq = sb("sess_sq", [P, D])
        sess_n = sb("sess_n", [P, 4])
        sel = sb("sel", [P, D])
        selT = sb("selT", [P, P])
        mask = sb("mask", [P, KB * L])
        seq_idx = sb("seq_idx", [P, KB * L], I32)
        sq = seq[:, 0, :, :].rearrange("p l d -> p (l d)")
        tiles_sb = seq[:, 1, :, :].rearrange("p l d -> p (l d)").bitcast(I32)[:, 0:SC * 3 * P].rearrange(
            "p (k f e) -> p k f e", k=SC, f=3)
        ids_i = seq[:, 1, :, :].rearrange("p l d -> p (l d)").bitcast(I32)[:, 3 * SC * P:3 * SC * P + 3 * KB * L].rearrange(
            "p (f k l) -> p f k l", f=3, k=KB)
        items_f = sq[:, 4700:4700 + KB * L].rearrange("p (k l) -> p k l", k=KB)
        alias_f = sq[:, 5100:5100 + KB * L]
        seq_idx_f = sq[:, 5500:5500 + KB * L]
        pick = sq[:, 5900:5900 + L]
        iota50 = sq[:, 6000:6000 + L]
        keyb = sq[:, 0:TILES]
        key_f = sq[0:1, 2048:2048 + TILES]
        key_i = sq[0:1, 4096:4096 + TILES].bitcast(I32)
        junk = sq[:, 2048:2048 + TILES]
        tile_no = seq[0:1, 1, :, :].rearrange("p l d -> p (l d)").bitcast(I32)[:, 0:TILES]

        ps_big = pb("ps_big", [P, 4, 512])
        ps_tab = pb("ps_tab", [P, 2, 512])
        ps_iota = pb("ps_iota", [P, 512])
        ps_misc = pb("ps_misc", [P, 512])
        ps_x = ps_tab
        ps_w = ps_iota
        ps_g = ps_big[:, 0:2, :]
        ps_s = ps_big[:, 2:4, :]
        beta_ps = ps_misc[:, 0:L]
        hsT_ps = ps_misc[:, 64:64 + P]
        hg_ps = ps_misc[:, 64 + P:64 + 2 * P]
        selT_ps = ps_misc[:, 64 + 2 * P:64 + 3 * P]
        graphT = sumA[:].rearrange("p b f -> p (b f)")
        nh = sumB[:].rearrange("p b f -> p (b f)")[:, 0:L * P]
        iota_ps = ps_iota[:, 0:BLOCK]

        key_landed = sem("key_landed")
        edges_stored = sem("edges_stored")
        pad_made = sem("pad_made")
        ids_landed = sem("ids_landed")
        e_landed = sem("e_landed")
        e_first_half = sem("e_first_half")
        iotas_made = sem("iotas_made")
        ident_zero = sem("ident_zero")
        ident_made = sem("ident_made")
        ones_made = sem("ones_made")
        prep = sem("prep")
        key_made = sem("key_made")
        key_spread = sem("key_spread")
        key_copied = sem("key_copied")
        tile_of_step = sem("tile_of_step")
        tiles_landed = [sem(f"tiles_landed{k}") for k in range(SC)]
        table_f = sem("table_f")
        table_T = sem("table_T")
        table_out_a = sem("table_out_a")
        table_out_v = sem("table_out_v")
        iota_ready = sem("iota_ready")
        idx_ready = sem("idx_ready")
        gathered = [sem(f"gathered{i}") for i in range(RING)]
        onehot_made = sem("onehot_made")
        steps_done = sem("steps_done")
        added = sem("added")
        picked = sem("picked")
        e_added = sem("e_added")
        squared = sem("squared")
        ssq_made = sem("ssq_made")
        nrm_made = sem("nrm_made")
        tail_v = sem("tail_v")
        h_ready = sem("h_ready")
        h_stored = sem("h_stored")
        g_stored = sem("g_stored")
        seq_idx_ready = sem("seq_idx_ready")
        g_thirds = sem("g_thirds")

        weights_landed = sem("weights_landed")
        weights_T = sem("weights_T")
        weights_out = sem("weights_out")
        pos_product = sem("pos_product")
        pos_out = sem("pos_out")
        graph_sq = sem("graph_sq")
        graph_ssq = sem("graph_ssq")
        graph_nrm = sem("graph_nrm")
        graph_unit = sem("graph_unit")
        graph_T = sem("graph_T")
        graph_out = [sem("graph_out0"), sem("graph_out1")]
        cur_seq_made = sem("cur_seq_made")
        seq_landed = [[sem(f"seq_landed{p}_{g}") for g in range(-(-L // 4))] for p in range(2)]
        x_ready = sem("x_ready")
        x_copied = sem("x_copied")
        w_ready = sem("w_ready")
        tanh_done = sem("tanh_done")
        hs_chain = sem("hs_chain")
        hs_ready = sem("hs_ready")
        hsT_ready = sem("hsT_ready")
        hsT_copied = sem("hsT_copied")
        hg_ready = sem("hg_ready")
        hg_copied = sem("hg_copied")
        g_ready = sem("g_ready")
        z_made = sem("z_made")
        gate_made = sem("gate_made")
        beta_ready = sem("beta_ready")
        beta_copied = sem("beta_copied")
        sess_chain = sem("sess_chain")
        sess_ssq = sem("sess_ssq")
        sess_nrm = sem("sess_nrm")
        sel_chain = sem("sel_chain")
        sel_ready = sem("sel_ready")
        selT_ready = sem("selT_ready")
        selT_copied = sem("selT_copied")
        scored = sem("scored")
        scores_out = [sem("scores_out0"), sem("scores_out1")]
        stored = [sem(f"stored{i}") for i in range(STAGES)]

        DONE0 = RING
        ADD0 = SLOTS
        CH = 7
        CB = NB // CH
        assert CB * CH == NB

        def edges(eng, body):
            with eng.Fori(0, LOOPS) as r:
                body(r * BODY, BODY, r)
            body(LOOPS * BODY, TAIL, None)

        def sessions(body):
            def run(eng):
                body(0, 0, 0)
                with eng.Fori(0, (KB - 2) // 2) as j:
                    body(j * 2 + 1, j, 1)
                    body(j * 2 + 2, j + 1, 0)
                body(KB - 1, (KB - 1) // 2, (KB - 1) % 2)
            return run

        def wait(eng, s, count):
            if not (isinstance(count, int) and count <= 0):
                eng.wait_ge(s, count)

        def width(c):
            return min(NC, N - c * NC)

        def score_slot(kap, par, c):
            return (NCH * par + c) % 2, kap * NCH + (NCH * par + c) // 2

        assert NCH % 2 == 1 and NG % 2 == 1
        block = ctx.enter_context(nc.Block())

        @block.sync
        def _(sp):
            sp.dma_start(key_i[:, 0:FULL], adj_row[P - 1:FULL * P:P].rearrange("(a n) -> a n", a=1),
                         allow_slow_non_contiguous=True).then_inc(key_landed, 16)
            for f, arr in enumerate((adj_row, adj_col, adj_val)):
                a = arr if f < 2 else arr.bitcast(I32)
                sp.dma_start(edge_tiles[0:FULL, f, :], a[0:FULL * P].rearrange("(t e) -> t e", e=P)).then_inc(edges_stored, 16)
                sp.dma_start(edge_tiles[FULL, f, 0:REST], a[FULL * P:NNZ]).then_inc(edges_stored, 16)
            sp.wait_ge(pad_made, 3)
            sp.dma_start(edge_tiles[FULL:FULL + 1, :, REST:P], pad[0:1, :, 0:P - REST]).then_inc(edges_stored, 16)
            sp.dma_start(edge_tiles[FULL + 1:FULL + 2, :, :], pad[0:1, :, :]).then_inc(edges_stored, 16)
            for i, arr in enumerate((items, inputs, alias)):
                sp.dma_start(ids_i[:, i, :, :], arr.rearrange("(k p) l -> p k l", p=P)).then_inc(ids_landed, 16)
            sp.dma_start(w1_sb[:], w1.rearrange("(a p) d -> p a d", p=P)).then_inc(weights_landed, 16)
            sp.dma_start(w2_sb[:], w2).then_inc(weights_landed, 16)
            sp.dma_start(glu_sb[:, 0, :], glu1_w).then_inc(weights_landed, 16)
            sp.dma_start(glu_sb[:, 1, :], glu2_w).then_inc(weights_landed, 16)
            sp.dma_start(b1_sb[:], glu1_b.rearrange("(p a) -> p a", a=1)).then_inc(weights_landed, 16)
            sp.dma_start(pos_sb[:], pos_emb).then_inc(weights_landed, 16)
            for c in range(CH):
                sp.wait_ge(h_ready, c + 1)
                sp.dma_start(h1_dram[c * CB * BLOCK:(c + 1) * CB * BLOCK, :].rearrange("(j p) d -> p j d", p=P),
                             sumA[:, c * CB:(c + 1) * CB, :].rearrange("p b (h d) -> p (b h) d", h=HALVES)).then_inc(h_stored, 16)
            sp.dma_start(e_rows[:], E[0:BLOCK, :].rearrange("(h p) d -> p h d", p=P)).then_inc(e_landed, 16)
            with sp.Fori(1, NB - 1) as b:
                sp.wait_ge(e_added, b)
                sp.dma_start(e_rows[:], E[bass.ds(b * BLOCK, BLOCK), :].rearrange("(h p) d -> p h d", p=P)).then_inc(e_landed, 16)
            sp.wait_ge(e_added, NB - 1)
            last = N - (NB - 1) * BLOCK - P
            sp.dma_start(e_rows[:, 0, :], E[(NB - 1) * BLOCK:(NB - 1) * BLOCK + P, :]).then_inc(e_first_half, 16)
            sp.wait_ge(e_first_half, 16)
            sp.dma_start(e_rows[0:last, 1, :], E[(NB - 1) * BLOCK + P:N, :]).then_inc(e_landed, 16)
            for c in range(CH):
                sp.wait_ge(g_thirds, c + 1)
                sp.dma_start(graph_dram[c * CB * BLOCK:(c + 1) * CB * BLOCK, :].rearrange("(j p) d -> p j d", p=P),
                             sumA[:, c * CB:(c + 1) * CB, :].rearrange("p b (h d) -> p (b h) d", h=HALVES)).then_inc(g_stored, 16)

            def store(k, kap, par):
                for u in range(PAIRS):
                    cs = [c for c in (2 * u, 2 * u + 1) if c < NCH]
                    for c in cs:
                        bank, before = score_slot(kap, par, c)
                        sp.wait_ge(scores_out[bank], before + 1)
                    n0, n1 = cs[0] * NC, min(N, (cs[-1] + 1) * NC)
                    sp.dma_start(out[bass.ds(k * P, P), n0:n1], stage[:, u % STAGES, 0:n1 - n0]).then_inc(stored[u % STAGES], 16)
            sessions(store)(sp)
            for i in range(STAGES):
                sp.wait_ge(stored[i], 16 * USES[i] * KB)

        @block.gpsimd
        def _(pool):
            pool.memset(pad[:, 0, :], NOWHERE).then_inc(pad_made, 1)
            pool.memset(pad[:, 1, :], 0).then_inc(pad_made, 1)
            pool.memset(pad[:, 2, :], 0).then_inc(pad_made, 1)
            pool.iota(tile_no, pattern=[[1, TILES]], base=0, channel_multiplier=0).then_inc(iotas_made, 1)
            pool.iota(scol_i[:], pattern=[[P, SC]], base=0, channel_multiplier=1).then_inc(iotas_made, 1)
            pool.iota(iota_i[:], pattern=[[1, BLOCK]], base=0, channel_multiplier=0).then_inc(iotas_made, 1)
            pool.memset(ident[:], 0.0).then_inc(ident_zero, 1)
            pool.wait_ge(ident_zero, 1)
            pool.affine_select(out=ident[:], in_=ident[:], compare_op=ALU.not_equal, fill=1.0, base=0,
                               pattern=[[-1, P]], channel_multiplier=1).then_inc(ident_made, 1)
            pool.wait_ge(edges_stored, 16 * 8)
            for k in range(SC):
                pool.wait_ge(tile_of_step, k + 1)
                pool.indirect_dma_start(tiles_sb[:, k, :, :].rearrange("p f e -> p (f e)"), None,
                                        edge_tiles.rearrange("t f e -> t (f e)"),
                                        bass.IndirectOffsetOnAxis(ap=tcol_i[:, k:k + 1], axis=0)).then_inc(tiles_landed[k], 16)
            for rnd in range(LAYERS):
                src = E if rnd == 0 else h1_dram
                if rnd == 1:
                    pool.wait_ge(h_stored, 16 * CH)

                def body(s0, n, r):
                    for q in range(n // GROUP):
                        pool.wait_ge(idx_ready, rnd * (STEPS // GROUP) + (s0 // GROUP if r is None else r * (BODY // GROUP)) + q + 1)
                        pool.nop(nofuse=True)
                        for i in range(q * GROUP, (q + 1) * GROUP):
                            slot = i % RING
                            pool.indirect_dma_start(ring[:, slot, :], None, src[:, :],
                                                    bass.IndirectOffsetOnAxis(ap=cur[:, slot:slot + 1], axis=0)).then_inc(gathered[slot], 16)
                edges(pool, body)

            pool.wait_ge(g_stored, 16 * CH)
            pool.wait_ge(seq_idx_ready, 1)

            def gather(k, kap, par):
                wait(pool, sess_chain, (k - 1) * L)
                pool.tensor_copy(cur_seq[:, par, :], seq_idx[:, bass.ds(k * L, L)]).then_inc(cur_seq_made, 1)
                pool.wait_ge(cur_seq_made, k + 1)
                pool.nop(nofuse=True)
                for l in range(L):
                    pool.indirect_dma_start(seq[:, par, l, :], None, graph_dram[:, :],
                                            bass.IndirectOffsetOnAxis(ap=cur_seq[:, par, l:l + 1], axis=0)).then_inc(seq_landed[par][l // 4], 16)
            sessions(gather)(pool)

        @block.scalar
        def _(act):
            for c in range(4):
                w = min(512, TILES - 512 * c)
                act.wait_ge(key_spread, c + 1)
                act.activation(keyb[:, 512 * c:512 * c + w], ps_big[:, c, 0:w], ACT.Copy).then_inc(key_copied, 1)
            act.wait_ge(iotas_made, 3)
            act.activation(iota_ps, iota_i[:], ACT.Copy).then_inc(iota_ready, 1)
            for k in range(0, SC, 2):
                at = slice(k * P, (k + 1) * P)
                act.wait_ge(table_T, k + 1)
                act.activation(colT[:, at], ps_tab[:, 0, 0:P], ACT.Copy)
                act.activation(valT[:, at], ps_tab[:, 0, P:2 * P], ACT.Copy)
                act.activation(rowT[:, at], ps_tab[:, 0, 2 * P:3 * P], ACT.Copy)
                act.activation(block_of[:, at], ps_tab[0:1, 0, 3 * P:4 * P], ACT.Copy).then_inc(table_out_a, 1)
            act.wait_ge(table_out_a, -(-SC // 2))
            act.wait_ge(table_out_v, SC // 2)
            for rnd in range(LAYERS):
                def body(s0, n, r):
                    for q in range(n // GROUP):
                        act.wait_ge(steps_done, rnd * STEPS + s0 + (q + 1) * GROUP)
                        at = (q * GROUP) % RING
                        act.activation(cur[:, at:at + GROUP], colT[:, bass.ds(s0 + q * GROUP, GROUP)], ACT.Copy).then_inc(idx_ready, 1)
                edges(act, body)
                for c in range(CH):
                    src = (sumA, sumB)[rnd]
                    if c == 0:
                        act.wait_ge(added, ADD0 + (rnd + 1) * STEPS)
                    if c >= 2:
                        act.wait_ge(ssq_made, rnd * CH + c - 1)
                    w = CB * BLOCK
                    act.activation(sq[:, (c % 2) * w:(c % 2 + 1) * w], src[:, c * CB:(c + 1) * CB, :].rearrange("p b f -> p (b f)"),
                                   ACT.Square).then_inc(squared, 1)
                act.wait_ge(ssq_made, (rnd + 1) * CH)
                act.activation(nrm[:], ssq[:], ACT.Sqrt).then_inc(nrm_made, 1)
            for c in range(CH):
                act.wait_ge(h_ready, CH + c + 1)
                v = sumA[:, c * CB:(c + 1) * CB, :].rearrange("p b f -> p (b f)")
                act.activation(v, v, ACT.Copy, scale=1.0 / (LAYERS + 1)).then_inc(g_thirds, 1)
            for c in range(CH):
                act.wait_ge(g_thirds, c + 1)
                v = sumA[:, c * CB:(c + 1) * CB, :].rearrange("p b f -> p (b f)")
                act.activation(sumB[:, c * CB:(c + 1) * CB, :].rearrange("p b f -> p (b f)"), v, ACT.Square).then_inc(graph_sq, 1)
            act.wait_ge(graph_ssq, CH)
            act.activation(nrm[:], ssq[:], ACT.Sqrt).then_inc(graph_nrm, 1)
            for q in range(1, NCH, 2):
                act.wait_ge(graph_T, q + 1)
                w = min(4, NJ - 4 * q) * P
                act.activation(graphT[:, q * NC:q * NC + w], ps_big[:, q % 4, 0:w], ACT.Copy).then_inc(graph_out[1], 1)

            def evacuate(k, kap, par, c):
                bank, before = score_slot(kap, par, c)
                if bank == 1:
                    act.wait_ge(scored, k * NCH + c + 1)
                    u = c // 2
                    wait(act, stored[u % STAGES], (k * USES[u % STAGES] + u // STAGES) * 16)
                    act.activation(stage[:, u % STAGES, c % 2 * NC:c % 2 * NC + width(c)], ps_s[:, 1, 0:width(c)], ACT.Copy)\
                        .then_inc(scores_out[1], 1)

            def root(k):
                act.wait_ge(sess_ssq, k + 1)
                act.activation(sess_n[:, 1:2], sess_n[:, 0:1], ACT.Sqrt).then_inc(sess_nrm, 1)

            def batch(k, kap, par):
                first = isinstance(k, int) and k == 0
                for g in range(NG):
                    n = k * NG + g
                    act.wait_ge(w_ready, n + 1)
                    wait(act, g_ready, n - NG + 1)
                    for j in range(GS[g]):
                        l = 4 * g + j
                        t = act.activation(nh[:, l * P:(l + 1) * P], ps_w[:, j * P:(j + 1) * P], ACT.Tanh,
                                           bias=posW[:, L - 1 - l:L - l])
                    t.then_inc(tanh_done, 1)
                    if not first:
                        if g == 3:
                            root(k - 1)
                        for c in CHUNKS[g]:
                            evacuate(k - 1, kap if par else kap - 1, 1 - par, c)
                for g in range(NG):
                    n = k * NG + g
                    act.wait_ge(z_made, n + 1)
                    wait(act, beta_ready, n - 1)
                    w = GS[g] * P
                    act.activation(gate[:, (par + g) % 2, 0:w], z[:, (par + g) % 2, 0:w], ACT.Sigmoid).then_inc(gate_made, 1)

            act.wait_ge(graph_T, NCH)
            sessions(batch)(act)
            root(KB - 1)
            for c in range(NCH):
                evacuate(KB - 1, (KB - 1) // 2, (KB - 1) % 2, c)

        @block.tensor
        def _(pe):
            pe.wait_ge(key_made, 1)
            pe.wait_ge(ones_made, 1)
            for c in range(4):
                w = min(512, TILES - 512 * c)
                pe.matmul(ps_big[:, c, 0:w], ones[:], key_f[:, 512 * c:512 * c + w], start=True, stop=True).then_inc(key_spread, 1)
            pe.wait_ge(ident_made, 1)
            for k in range(SC):
                pe.wait_ge(table_f, k + 1)
                if k >= 2:
                    pe.wait_ge((table_out_a, table_out_v)[k % 2], k // 2)
                pe.transpose(ps_tab[:, k % 2, 0:P], tiles_sb[:, k, 1, :].bitcast(F32), ident[:])
                pe.transpose(ps_tab[:, k % 2, P:2 * P], tiles_sb[:, k, 2, :].bitcast(F32), ident[:])
                pe.transpose(ps_tab[:, k % 2, 2 * P:3 * P], tiles_sb[:, k, 0, :].bitcast(F32), ident[:])
                pe.matmul(ps_tab[0:1, k % 2, 3 * P:4 * P], bcol[:, k:k + 1], ident[:], start=True, stop=True).then_inc(table_T, 1)
            pe.wait_ge(weights_landed, 16 * 6)
            pe.transpose(ps_misc[:, 0:L], pos_sb[:], ident[0:L, 0:L])
            for i in range(2):
                t = pe.transpose(ps_misc[:, 64 + i * P:64 + (i + 1) * P], glu_sb[:, i, :], ident[:])
            t.then_inc(weights_T, 1)
            pe.wait_ge(weights_out, 1)
            pe.matmul(ps_misc[:, 0:L], w1_sb[:, 0, :], posT[:], start=True, stop=True).then_inc(pos_product, 1)
            pe.wait_ge(key_copied, 4)
            for rnd in range(LAYERS):
                def body(s0, n, r):
                    for i in range(n):
                        slot = i % RING
                        pe.wait_ge(onehot_made, rnd * (STEPS + 1) + s0 + i + 1)
                        lap = (r * (BODY // RING) if r is not None else LOOPS * BODY // RING) + i // RING
                        pe.wait_ge(gathered[slot], (lap + rnd * LAPS + 1) * 16)
                        pe.wait_ge(added, rnd * STEPS + s0 + i + 1)
                        for h in range(HALVES):
                            mm = pe.matmul(ps_big[:, i % SLOTS, h * D:(h + 1) * D], onehot[:, i % SLOTS, h * P:(h + 1) * P],
                                           ring[:, slot, :], start=True, stop=True)
                        mm.then_inc(steps_done, 1)
                edges(pe, body)

            pe.wait_ge(g_stored, 16 * CH)
            for q in range(NCH):
                if q >= 4:
                    pe.wait_ge(graph_out[q % 2], q // 2 - 1)
                for i in range(min(4, NJ - 4 * q)):
                    j = 4 * q + i
                    if j % (CB * HALVES) == 0:
                        pe.wait_ge(graph_unit, j // (CB * HALVES) + 1)
                    b, h = j // HALVES, j % HALVES
                    t = pe.transpose(ps_big[:, q % 4, i * P:(i + 1) * P], sumB[:, b, h * D:(h + 1) * D], ident[:])
                t.then_inc(graph_T, 1)
            pe.wait_ge(graph_out[0], -(-NCH // 2))
            pe.wait_ge(graph_out[1], NCH // 2)

            def turn(k, kap, par, g):
                n = k * NG + g
                pe.wait_ge(seq_landed[par][g], (kap + 1) * (GS[g] * 16))
                wait(pe, x_copied, n - 1)
                for j in range(GS[g]):
                    t = pe.transpose(ps_x[:, (par + g) % 2, j * P:(j + 1) * P], seq[:, par, 4 * g + j, :], ident[:])
                t.then_inc(x_ready, 1)

            def product(k, par, g):
                n = k * NG + g
                pe.wait_ge(x_copied, n + 1)
                wait(pe, tanh_done, n)
                w = GS[g] * P
                pe.matmul(ps_w[:, 0:w], w1_sb[:, 1, :], xT[:, (par + g) % 2, 0:w], start=True, stop=True).then_inc(w_ready, 1)

            def gates(k, par, g):
                n = k * NG + g
                pe.wait_ge(tanh_done, n + 1)
                wait(pe, z_made, n - 1)
                w = GS[g] * P
                pe.matmul(ps_g[:, (par + g) % 2, 0:w], gluT[:, 0, :], nh[:, 4 * g * P:4 * g * P + w], start=True, stop=True)\
                    .then_inc(g_ready, 1)

            def weigh(k, par, g):
                pe.wait_ge(gate_made, k * NG + g + 1)
                for j in range(GS[g]):
                    l = 4 * g + j
                    t = pe.matmul(beta_ps[:, l:l + 1], gate[:, (par + g) % 2, j * P:(j + 1) * P], w2_sb[:], start=True, stop=True)
                t.then_inc(beta_ready, 1)

            def turn_sel(k):
                pe.wait_ge(sel_ready, k + 1)
                pe.transpose(selT_ps, sel[:], ident[:]).then_inc(selT_ready, 1)

            def score(k, kap, par, c):
                if c == 0:
                    pe.wait_ge(selT_copied, k + 1)
                bank, before = score_slot(kap, par, c)
                wait(pe, scores_out[bank], before)
                pe.matmul(ps_s[:, bank, 0:width(c)], selT[:], graphT[:, c * NC:c * NC + width(c)], start=True, stop=True)\
                    .then_inc(scored, 1)

            def batch(k, kap, par):
                first = isinstance(k, int) and k == 0
                turn(k, kap, par, 0)
                for g in range(NG):
                    if g + 1 < NG:
                        turn(k, kap, par, g + 1)
                    product(k, par, g)
                    if not first:
                        if g == 4:
                            turn_sel(k - 1)
                        for c in CHUNKS[g]:
                            score(k - 1, kap if par else kap - 1, 1 - par, c)
                pe.wait_ge(hs_ready, k + 1)
                pe.transpose(hsT_ps, hs[:], ident[:]).then_inc(hsT_ready, 1)
                pe.wait_ge(hsT_copied, k + 1)
                pe.matmul(hg_ps, gluT[:, 1, :], hsT[:], start=True, stop=True).then_inc(hg_ready, 1)
                gates(k, par, 0)
                for g in range(NG):
                    if g + 1 < NG:
                        gates(k, par, g + 1)
                    weigh(k, par, g)

            sessions(batch)(pe)
            turn_sel(KB - 1)
            for c in range(NCH):
                score(KB - 1, (KB - 1) // 2, (KB - 1) % 2, c)

        @block.vector
        def _(dve):
            links = [0]

            def link(ins):
                links[0] += 1
                ins.then_inc(prep, 1)
                dve.wait_ge(prep, links[0])

            dve.memset(ones[:], 1.0).then_inc(ones_made, 1)
            dve.wait_ge(key_landed, 16)
            dve.wait_ge(iotas_made, 2)
            link(dve.tensor_scalar(key_i[:, 0:FULL], key_i[:, 0:FULL], BLOCK.bit_length() - 1, None, ALU.arith_shift_right))
            link(dve.memset(key_i[:, FULL:TILES], NB - 1))
            dve.tensor_tensor(key_f, key_i, tile_no, ALU.add).then_inc(key_made, 1)
            link(dve.tensor_copy(scol[:], scol_i[:]))
            dve.wait_ge(key_copied, 4)
            for k in range(SC):
                link(dve.tensor_scalar(junk, keyb, scol[:, k:k + 1], 0.0, ALU.is_lt, ALU.add, accum_out=tcol[:, k:k + 1]))
                dve.tensor_copy(tcol_i[:, k:k + 1], tcol[:, k:k + 1]).then_inc(tile_of_step, 1)
            link(dve.tensor_tensor(bcol[:], scol[:], tcol[:], ALU.subtract))
            link(dve.tensor_scalar(bcol[:], bcol[:], float(NB - 1), None, ALU.min))
            link(dve.tensor_scalar(b256[:], bcol[:], float(BLOCK), None, ALU.mult))

            def table_out(k):
                dve.wait_ge(table_T, k + 1)
                at = slice(k * P, (k + 1) * P)
                dve.tensor_copy(colT[:, at], ps_tab[:, 1, 0:P])
                dve.tensor_copy(valT[:, at], ps_tab[:, 1, P:2 * P])
                dve.tensor_copy(rowT[:, at], ps_tab[:, 1, 2 * P:3 * P])
                dve.tensor_copy(block_of[:, at], ps_tab[0:1, 1, 3 * P:4 * P]).then_inc(table_out_v, 1)

            for k in range(SC):
                dve.wait_ge(tiles_landed[k], 16)
                dve.tensor_copy(tiles_sb[:, k, 1, :].bitcast(F32), tiles_sb[:, k, 1, :])
                dve.tensor_scalar(tiles_sb[:, k, 0, :].bitcast(F32), tiles_sb[:, k, 0, :], b256[:, k:k + 1], None,
                                  ALU.subtract).then_inc(table_f, 1)
                if k % 2 == 0 and k >= 2:
                    table_out(k - 1)
            if SC % 2 == 0:
                table_out(SC - 1)
            dve.wait_ge(table_out_v, SC // 2)
            dve.wait_ge(table_out_a, -(-SC // 2))
            dve.wait_ge(iota_ready, 1)
            dve.wait_ge(weights_T, 1)
            dve.tensor_copy(posT[:], ps_misc[:, 0:L])
            dve.tensor_copy(gluT[:].rearrange("p a d -> p (a d)"), ps_misc[:, 64:64 + 2 * P]).then_inc(weights_out, 1)
            dve.wait_ge(pos_product, 1)
            dve.tensor_copy(posW[:], ps_misc[:, 0:L]).then_inc(pos_out, 1)
            link(dve.memset(sumB[:], 0.0))
            dve.memset(sumA[:], 0.0).then_inc(added, ADD0)
            dve.wait_ge(ids_landed, 48)
            link(dve.tensor_scalar(items_f[:], ids_i[:, 0, :, :], float(N - 1), 0.0, ALU.min, ALU.max))
            link(dve.tensor_scalar(mask[:], ids_i[:, 1, :, :].rearrange("p k l -> p (k l)"), 0.0, None, ALU.not_equal))
            link(dve.tensor_reduce(rcnt[:], mask[:].rearrange("p (k l) -> p k l", l=L), AX_X, ALU.add))
            link(dve.reciprocal(rcnt[:], rcnt[:]))
            link(dve.tensor_copy(alias_f[:], ids_i[:, 2, :, :].rearrange("p k l -> p (k l)")))
            link(dve.tensor_copy(iota50, iota_i[:, 0:L]))
            dve.memset(pick, 0.0).then_inc(steps_done, DONE0)

            def pick_items(l):
                for k in range(KB):
                    dve.wait_ge(picked, l * KB + k)
                    at = k * L + l
                    dve.scalar_tensor_tensor(out=pick, in0=iota50, scalar=alias_f[:, bass.ds(at, 1)], in1=items_f[:, k, :],
                                             op0=ALU.is_equal, op1=ALU.mult, accum_out=seq_idx_f[:, bass.ds(at, 1)]).then_inc(picked, 1)

            for rnd in range(LAYERS):
                acc = (sumA, sumB)[rnd]
                accf = acc[:].rearrange("p b f -> p (b f)")

                def make_onehot(s, slot):
                    dve.wait_ge(steps_done, rnd * STEPS + s + 1 + DONE0 - SLOTS)
                    dve.tensor_scalar(onehot[:, slot, :], iota_ps, rowT[:, bass.ds(s, 1)], valT[:, bass.ds(s, 1)],
                                      ALU.is_equal, ALU.mult).then_inc(onehot_made, 1)

                def body(s0, n, r):
                    for i in range(n):
                        make_onehot(s0 + i + 1, (i + 1) % SLOTS)
                        b = dve.value_load(block_of[0:1, bass.ds(s0 + i, 1)], min_val=0, max_val=NB - 1)
                        dve.wait_ge(steps_done, rnd * STEPS + s0 + i + 1 + DONE0)
                        dve.wait_ge(added, rnd * STEPS + s0 + i + ADD0)
                        dst = accf[:, bass.ds(b * BLOCK, BLOCK)]
                        dve.tensor_tensor(dst, dst, ps_big[:, i % SLOTS, 0:BLOCK], ALU.add).then_inc(added, 1)
                    if rnd == 0:
                        if r is not None:
                            with_l = r
                            pick_items(with_l)
                        else:
                            for l in range(LOOPS, L):
                                pick_items(l)
                            dve.wait_ge(picked, KB * L)
                            dve.tensor_copy(seq_idx[:], seq_idx_f[:]).then_inc(seq_idx_ready, 1)
                    if rnd == 1 and r is not None:
                        dve.wait_ge(e_landed, r * 16 + 16)
                        dst = sumA[:].rearrange("p b f -> p (b f)")[:, bass.ds(r * BLOCK, BLOCK)]
                        dve.tensor_tensor(dst, dst, e_rows[:].rearrange("p h d -> p (h d)"), ALU.add).then_inc(e_added, 1)

                make_onehot(0, 0)
                edges(dve, body)
                for c in range(CH):
                    w = CB * BLOCK
                    dve.wait_ge(squared, rnd * CH + c + 1)
                    dve.tensor_reduce(ssq[:, c * CB * HALVES:(c + 1) * CB * HALVES],
                                      sq[:, (c % 2) * w:(c % 2 + 1) * w].rearrange("p (j d) -> p j d", d=D), AX_X, ALU.add).then_inc(ssq_made, 1)
                dve.wait_ge(nrm_made, rnd + 1)
                dve.tensor_scalar(nrm[:], nrm[:], EPS, None, ALU.max).then_inc(tail_v, 1)
                dve.wait_ge(tail_v, 2 * rnd + 1)
                dve.reciprocal(inv[:], nrm[:]).then_inc(tail_v, 1)
                dve.wait_ge(tail_v, 2 * rnd + 2)
                for j in range(NJ):
                    b, h = j // HALVES, j % HALVES
                    src = acc[:, b, h * D:(h + 1) * D]
                    if rnd == 0:
                        ins = dve.tensor_scalar(src, src, inv[:, j:j + 1], None, ALU.mult)
                    else:
                        dst = sumA[:, b, h * D:(h + 1) * D]
                        ins = dve.scalar_tensor_tensor(out=dst, in0=src, scalar=inv[:, j:j + 1], in1=dst, op0=ALU.mult, op1=ALU.add)
                    if (j + 1) % (CB * HALVES) == 0:
                        ins.then_inc(h_ready, 1)

            for c in range(CH):
                w = CB * BLOCK
                dve.wait_ge(graph_sq, c + 1)
                dve.tensor_reduce(ssq[:, c * CB * HALVES:(c + 1) * CB * HALVES],
                                  sumB[:, c * CB:(c + 1) * CB, :].rearrange("p b (h d) -> p (b h) d", d=D), AX_X, ALU.add).then_inc(graph_ssq, 1)
            dve.wait_ge(graph_nrm, 1)
            dve.tensor_scalar(nrm[:], nrm[:], EPS, None, ALU.max).then_inc(tail_v, 1)
            dve.wait_ge(tail_v, 2 * LAYERS + 1)
            dve.reciprocal(inv[:], nrm[:]).then_inc(tail_v, 1)
            dve.wait_ge(tail_v, 2 * LAYERS + 2)
            for j in range(NJ):
                b, h = j // HALVES, j % HALVES
                ins = dve.tensor_scalar(sumB[:, b, h * D:(h + 1) * D], sumA[:, b, h * D:(h + 1) * D], inv[:, j:j + 1], None, ALU.mult)
                if (j + 1) % (CB * HALVES) == 0:
                    ins.then_inc(graph_unit, 1)
            for q in range(0, NCH, 2):
                dve.wait_ge(graph_T, q + 1)
                w = min(4, NJ - 4 * q) * P
                dve.tensor_copy(graphT[:, q * NC:q * NC + w], ps_big[:, q % 4, 0:w]).then_inc(graph_out[0], 1)

            def turned(k, par, g):
                n = k * NG + g
                dve.wait_ge(x_ready, n + 1)
                wait(dve, w_ready, n - 1)
                w = GS[g] * P
                dve.tensor_copy(xT[:, (par + g) % 2, 0:w], ps_x[:, (par + g) % 2, 0:w]).then_inc(x_copied, 1)

            def mean(k, kap, par, g):
                dve.wait_ge(seq_landed[par][g], (kap + 1) * (GS[g] * 16))
                for l in range(4 * g, 4 * g + GS[g]):
                    m = mask[:, bass.ds(k * L + l, 1)]
                    if l == 0:
                        wait(dve, hsT_ready, k)
                        t = dve.tensor_scalar(hs[:], seq[:, par, l, :], m, None, ALU.mult)
                    else:
                        dve.wait_ge(hs_chain, k * L + l)
                        t = dve.scalar_tensor_tensor(out=hs[:], in0=seq[:, par, l, :], scalar=m, in1=hs[:], op0=ALU.mult, op1=ALU.add)
                    t.then_inc(hs_chain, 1)

            def summed(k, par, l0, l1):
                if l0 == 0:
                    dve.wait_ge(beta_ready, (k + 1) * NG)
                    wait(dve, sess_chain, k * L)
                    dve.tensor_tensor(beta[:], beta_ps, mask[:, bass.ds(k * L, L)], ALU.mult).then_inc(beta_copied, 1)
                    dve.wait_ge(beta_copied, k + 1)
                for l in range(l0, l1):
                    if l == 0:
                        wait(dve, sel_ready, k)
                        t = dve.tensor_scalar(sess[:], seq[:, par, l, :], beta[:, l:l + 1], None, ALU.mult)
                    else:
                        dve.wait_ge(sess_chain, k * L + l)
                        t = dve.scalar_tensor_tensor(out=sess[:], in0=seq[:, par, l, :], scalar=beta[:, l:l + 1], in1=sess[:],
                                                     op0=ALU.mult, op1=ALU.add)
                    t.then_inc(sess_chain, 1)
                if l1 == L:
                    dve.wait_ge(sess_chain, (k + 1) * L)
                    dve.scalar_tensor_tensor(out=sess_sq[:], in0=sess[:], scalar=1.0, in1=sess[:], op0=ALU.mult, op1=ALU.mult,
                                             accum_out=sess_n[:, 0:1]).then_inc(sess_ssq, 1)

            def select(k):
                dve.wait_ge(sess_nrm, k + 1)
                dve.tensor_scalar(sess_n[:, 2:3], sess_n[:, 1:2], EPS, None, ALU.max).then_inc(sel_chain, 1)
                dve.wait_ge(sel_chain, k * 2 + 1)
                dve.reciprocal(sess_n[:, 3:4], sess_n[:, 2:3]).then_inc(sel_chain, 1)
                dve.wait_ge(sel_chain, k * 2 + 2)
                wait(dve, selT_ready, k)
                dve.tensor_scalar(sel[:], sess[:], sess_n[:, 3:4], W_K, ALU.mult, ALU.mult).then_inc(sel_ready, 1)

            def selected(k):
                dve.wait_ge(selT_ready, k + 1)
                wait(dve, scored, k * NCH)
                dve.tensor_copy(selT[:], selT_ps).then_inc(selT_copied, 1)

            def evacuate(k, kap, par, c):
                bank, before = score_slot(kap, par, c)
                if bank == 0:
                    dve.wait_ge(scored, k * NCH + c + 1)
                    u = c // 2
                    wait(dve, stored[u % STAGES], (k * USES[u % STAGES] + u // STAGES) * 16)
                    dve.tensor_copy(stage[:, u % STAGES, c % 2 * NC:c % 2 * NC + width(c)], ps_s[:, 0, 0:width(c)])\
                        .then_inc(scores_out[0], 1)

            THIRD = -(-L // 3)

            def batch(k, kap, par):
                first = isinstance(k, int) and k == 0
                turned(k, par, 0)
                for g in range(NG):
                    if g + 1 < NG:
                        turned(k, par, g + 1)
                    mean(k, kap, par, g)
                    if not first:
                        if g < 3:
                            summed(k - 1, 1 - par, g * THIRD, min(L, (g + 1) * THIRD))
                        if g == 3:
                            select(k - 1)
                        if g == 4:
                            selected(k - 1)
                        for c in CHUNKS[g]:
                            evacuate(k - 1, kap if par else kap - 1, 1 - par, c)
                dve.wait_ge(hs_chain, (k + 1) * L)
                dve.tensor_scalar(hs[:], hs[:], rcnt[:, bass.ds(k, 1)], None, ALU.mult).then_inc(hs_ready, 1)
                dve.wait_ge(hsT_ready, k + 1)
                dve.tensor_copy(hsT[:], hsT_ps).then_inc(hsT_copied, 1)
                dve.wait_ge(hg_ready, k + 1)
                dve.tensor_scalar(hgT[:], hg_ps, b1_sb[:], None, ALU.add).then_inc(hg_copied, 1)
                dve.wait_ge(hg_copied, k + 1)
                for g in range(NG):
                    n = k * NG + g
                    w = GS[g] * P
                    dve.wait_ge(g_ready, n + 1)
                    wait(dve, gate_made, n - 1)
                    dve.tensor_tensor(z[:, (par + g) % 2, 0:w].rearrange("p (j b) -> p j b", b=P),
                                      ps_g[:, (par + g) % 2, 0:w].rearrange("p (j b) -> p j b", b=P),
                                      hgT[:].unsqueeze(1).to_broadcast([P, GS[g], P]), ALU.add).then_inc(z_made, 1)

            dve.wait_ge(graph_out[1], NCH // 2)
            sessions(batch)(dve)
            summed(KB - 1, (KB - 1) % 2, 0, L)
            select(KB - 1)
            selected(KB - 1)
            for c in range(NCH):
                evacuate(KB - 1, (KB - 1) // 2, (KB - 1) % 2, c)


_INS = ['r_items', 'r_inputs', 'r_alias_inputs', 'L0_rec_adj_row', 'L0_rec_adj_col', 'L0_rec_adj_val', 'L0_rec_E',
        'L0_rec_pos_emb', 'L0_rec_w1', 'L0_rec_w2', 'L0_rec_glu1_w', 'L0_rec_glu1_b', 'L0_rec_glu2_w']
_OUTS = [((1024, 12500), 'float32')]


def kernel(**inputs):
    import numpy as _np
    import concourse.bacc as _bacc
    from concourse import mybir as _mybir
    from concourse.bass_utils import run_bass_kernel_spmd as _run

    nc = _bacc.Bacc("TRN2", target_bir_lowering=False, num_devices=1)
    arrays, args = {}, []
    for name in _INS:
        a = _np.ascontiguousarray(inputs[name])
        arrays[f"in_{name}_dram"] = a
        args.append(nc.dram_tensor(f"in_{name}_dram", a.shape, _mybir.dt.from_np(a.dtype), kind="ExternalInput").ap())
    for i, (shape, dtype) in enumerate(_OUTS):
        dt = _mybir.dt.from_np(_np.dtype(dtype))
        args.append(nc.dram_tensor(f"out_{i}_dram", shape, dt, kind="ExternalOutput").ap())
    rec_kernel(nc, *args)
    r = _run(nc, [arrays], core_ids=[0])
    return r.results[0]["out_0_dram"]
```

```python
from contextlib import ExitStack

import concourse.bass as bass
from concourse import mybir

ALU = mybir.AluOpType
ACT = mybir.ActivationFunctionType
AX_X = mybir.AxisListType.X
F32 = mybir.dt.float32
I32 = mybir.dt.int32

P = 128
LAYERS = 2
BLOCK = 128
TPC = 4
SLOTS = 8
BANKS = 4
UNROLL = 8
NOWHERE = 1 << 20
STAGES = 4
NC = 512
W_K = 12.0
EPS = 1e-12


def rec_kernel(nc, items, inputs, alias, adj_row, adj_col, adj_val, E, pos_emb, w1, w2, glu1_w, glu1_b, glu2_w, out):
    N, D = E.shape
    B, L = items.shape
    NNZ = adj_row.shape[0]
    FULL = NNZ // P
    REST = NNZ - FULL * P
    CHUNKS_E = -(-NNZ // (P * TPC))
    NB = -(-N // BLOCK)
    NP = NB * BLOCK
    STEPS = CHUNKS_E + NB - 1
    TC = -(-NNZ // (P * P))
    SC = -(-STEPS // P)
    LAPS = CHUNKS_E // SLOTS
    KB = B // P
    GS = [4] * (L // 4) + ([L % 4] if L % 4 else [])
    NG = len(GS)
    NCH = -(-N // NC)
    PAIRS = -(-NCH // 2)
    USES = [len(range(i, PAIRS, STAGES)) for i in range(STAGES)]
    C0 = 5
    SHARE = [0] * C0 + [NCH // (NG - C0) + (i < NCH % (NG - C0)) for i in range(NG - C0)]
    CHUNKS = [list(range(sum(SHARE[:g]), sum(SHARE[:g + 1]))) for g in range(NG)]
    LOOPS = STEPS // UNROLL
    FT = FULL % P
    assert 0 < REST < P and LOOPS * UNROLL == STEPS and D == P and TC * P >= CHUNKS_E * TPC
    assert FT and UNROLL % BANKS == 0 and UNROLL % 2 == 0 and L <= LOOPS and 2 * (LOOPS - NB // 2) >= 0

    h1_dram = nc.dram_tensor("h1_dram", (NP, D), F32, kind="Internal").ap()
    graph_dram = nc.dram_tensor("graph_dram", (NP, D), F32, kind="Internal").ap()

    with ExitStack() as ctx:
        def sb(name, shape, dt=F32):
            return ctx.enter_context(nc.sbuf_tensor(name, shape, dt))

        def sem(name):
            return ctx.enter_context(nc.semaphore(name))

        def pb(name, shape):
            return ctx.enter_context(nc.psum_tensor(name, shape, F32))

        sumA = sb("sumA", [P, NB, BLOCK])
        sumB = sb("sumB", [P, NB, BLOCK])
        seq = sb("seq", [P, 2, L, D])
        share3 = sb("share3", [P, 5 * SC * P])
        share1 = sb("share1", [P, max(STAGES * 2 * NC, (SLOTS + 2) * TPC * D)])
        ring = share1[:, 0:SLOTS * TPC * D]
        onehot = share1[:, SLOTS * TPC * D:(SLOTS + 2) * TPC * D].rearrange("p (s t f) -> p s t f", s=2, t=TPC)
        stage = share1[:, 0:STAGES * 2 * NC].rearrange("p (s f) -> p s f", s=STAGES)
        share2 = sb("share2", [P, max(2 * TC * P, 6 * NC)])
        rowT = share2[:, 0:TC * P]
        valT = share2[:, TC * P:2 * TC * P]
        xT = share2[:, 0:2 * NC].rearrange("p (s f) -> p s f", s=2)
        z = share2[:, 2 * NC:4 * NC].rearrange("p (s f) -> p s f", s=2)
        gate = share2[:, 4 * NC:6 * NC].rearrange("p (s f) -> p s f", s=2)
        colT = sb("colT", [P, TC * P], I32)
        slot_at = share3[0:1, 1 * SC * P:2 * SC * P].bitcast(I32)
        need_of = share3[0:1, 2 * SC * P:3 * SC * P].bitcast(I32)
        col_at = share3[0:1, 3 * SC * P:4 * SC * P].bitcast(I32)
        sum_at = share3[0:1, 4 * SC * P:5 * SC * P].bitcast(I32)
        free_at = sb("free_at", [1, SLOTS + CHUNKS_E], I32)
        first_row = share3[:, 0:SC * P]
        rel = sb("rel", [P, 2, TPC])
        cur = sb("cur", [P, SLOTS * TPC], I32)
        ident = sb("ident", [P, P])
        scol_i = sb("scol_i", [P, SC], I32)
        scol = sb("scol", [P, SC])
        ccol = sb("ccol", [P, SC])
        bcol = sb("bcol", [P, SC])
        ssq = sb("ssq", [P, NB])
        nrm = sb("nrm", [P, NB])
        inv = sb("inv", [P, NB])
        cur_seq = sb("cur_seq", [P, 2, L], I32)
        rcnt = sb("rcnt", [P, KB])
        w1_sb = sb("w1_sb", [P, 2, D])
        w2_sb = sb("w2_sb", [P, 1])
        gluT = sb("gluT", [P, 2, D])
        b1_sb = sb("b1_sb", [P, 1])
        posT = sb("posT", [P, L])
        posW = sb("posW", [P, L])
        hs = share3[:, 0 * P:1 * P]
        hsT = share3[:, 1 * P:2 * P]
        hgT = share3[:, 2 * P:3 * P]
        beta = sb("beta", [P, L])
        sess = share3[:, 3 * P:4 * P]
        sess_sq = share3[:, 4 * P:5 * P]
        sess_n = sb("sess_n", [P, 4])
        sel = share3[:, 5 * P:6 * P]
        selT = share3[:, 6 * P:7 * P]
        mask = sb("mask", [P, KB * L])
        seq_idx = sb("seq_idx", [P, KB * L], I32)
        sq = seq[:, 0, :, :].rearrange("p l d -> p (l d)")
        tiles_sb = seq[:, 1, :, :].rearrange("p l d -> p (l d)").bitcast(I32)[:, 0:TC * 3 * P].rearrange(
            "p (f k e) -> p f k e", k=TC, f=3)
        e_rows = seq[:].rearrange("p a l d -> p (a l d)")[:, 0:NB * D]
        ids_i = seq[:, 1, :, :].rearrange("p l d -> p (l d)").bitcast(I32)[:, 3 * TC * P:3 * TC * P + 3 * KB * L].rearrange(
            "p (f k l) -> p f k l", f=3, k=KB)
        items_f = sq[:, 4740:4740 + KB * L].rearrange("p (k l) -> p k l", k=KB)
        alias_f = sq[:, 5140:5140 + KB * L]
        seq_idx_f = sq[:, 5540:5540 + KB * L]
        pick = sq[:, 5940:5940 + L]
        iota50 = sq[:, 6000:6000 + L]
        glu_sb = sq[:, 4096:4096 + 2 * D].rearrange("p (a d) -> p a d", a=2)
        pos_sb = sq[0:L, 4352:4352 + D]
        last_one = sq[:, 4480:4480 + P]
        iota_i = sq[:, 4608:4608 + BLOCK].bitcast(I32)
        key_i = sq[:, 0:CHUNKS_E].bitcast(I32)
        key = sq[:, 512:512 + CHUNKS_E]
        chunk_no = sq[:, 1024:1024 + CHUNKS_E].bitcast(I32)
        stage_no = sq[:, 1536:1536 + SC * P].bitcast(I32)
        junk = sq[:, 2048:2048 + CHUNKS_E]
        spread = sq[:, 2560:2560 + SC * P].rearrange("p (k e) -> p k e", e=P)
        chunk_i = sq[0:1, 3584:3584 + SC * P].bitcast(I32)

        ps_big = pb("ps_big", [P, 4, 512])
        ps_tab = pb("ps_tab", [P, 2, 512])
        ps_iota = pb("ps_iota", [P, 512])
        ps_misc = pb("ps_misc", [P, 512])
        ps_x = ps_tab
        ps_w = ps_iota
        ps_g = ps_big[:, 0:2, :]
        ps_s = ps_big[:, 2:4, :]
        beta_ps = ps_misc[:, 0:L]
        hsT_ps = ps_misc[:, 64:64 + P]
        hg_ps = ps_misc[:, 64 + P:64 + 2 * P]
        selT_ps = ps_misc[:, 64 + 2 * P:64 + 3 * P]
        graphT = sumA[:].rearrange("p b f -> p (b f)")
        nh = sumB[:].rearrange("p b f -> p (b f)")[:, 0:L * P]
        iota_ps = ps_iota[:, 0:BLOCK]

        pads_made = sem("pads_made")
        edges_landed = [sem(f"edges_landed{f}") for f in range(3)]
        ids_landed = sem("ids_landed")
        e_landed = sem("e_landed")
        iotas_made = sem("iotas_made")
        ident_zero = sem("ident_zero")
        ident_made = sem("ident_made")
        last_made = sem("last_made")
        prep = sem("prep")
        tile_f = sem("tile_f")
        tile_T = sem("tile_T")
        tile_out = [sem("tile_out_v"), sem("tile_out_a")]
        last_rows = sem("last_rows")
        spread_made = sem("spread_made")
        blocks_ready = sem("blocks_ready")
        stage_tables = sem("stage_tables")
        iota_ready = sem("iota_ready")
        idx_ready = sem("idx_ready")
        gathered = [sem(f"gathered{i}") for i in range(SLOTS)]
        chunks_landed = sem("chunks_landed")
        onehot_made = sem("onehot_made")
        steps_done = sem("steps_done")
        added = sem("added")
        picked = sem("picked")
        rel_made = sem("rel_made")
        added_e = sem("added_e")
        squared = sem("squared")
        ssq_made = sem("ssq_made")
        nrm_made = sem("nrm_made")
        tail_v = sem("tail_v")
        h_ready = sem("h_ready")
        h_stored = sem("h_stored")
        g_stored = sem("g_stored")
        seq_idx_ready = sem("seq_idx_ready")
        g_thirds = sem("g_thirds")

        weights_landed = sem("weights_landed")
        weights_T = sem("weights_T")
        weights_out = sem("weights_out")
        pos_product = sem("pos_product")
        pos_out = sem("pos_out")
        graph_sq = sem("graph_sq")
        graph_ssq = sem("graph_ssq")
        graph_nrm = sem("graph_nrm")
        graph_unit = sem("graph_unit")
        graph_T = sem("graph_T")
        graph_out = [sem("graph_out0"), sem("graph_out1")]
        cur_seq_made = sem("cur_seq_made")
        seq_landed = [[sem(f"seq_landed{p}_{g}") for g in range(-(-L // 4))] for p in range(2)]
        x_ready = sem("x_ready")
        x_copied = sem("x_copied")
        w_ready = sem("w_ready")
        tanh_done = sem("tanh_done")
        hs_chain = sem("hs_chain")
        hs_ready = sem("hs_ready")
        hsT_ready = sem("hsT_ready")
        hsT_copied = sem("hsT_copied")
        hg_ready = sem("hg_ready")
        hg_copied = sem("hg_copied")
        g_ready = sem("g_ready")
        z_made = sem("z_made")
        gate_made = sem("gate_made")
        beta_ready = sem("beta_ready")
        beta_copied = sem("beta_copied")
        sess_chain = sem("sess_chain")
        sess_ssq = sem("sess_ssq")
        sess_nrm = sem("sess_nrm")
        sel_chain = sem("sel_chain")
        sel_ready = sem("sel_ready")
        selT_ready = sem("selT_ready")
        selT_copied = sem("selT_copied")
        scored = sem("scored")
        scores_out = [sem("scores_out0"), sem("scores_out1")]
        stored = [sem(f"stored{i}") for i in range(STAGES)]

        DONE0 = 2
        ADD0 = BANKS
        CH = 7
        CB = NB // CH
        assert CB * CH == NB

        def chunks(eng, body):
            with eng.Fori(0, LAPS) as lap:
                for i in range(SLOTS):
                    body(lap * SLOTS + i, lap, i)
            for i in range(CHUNKS_E - LAPS * SLOTS):
                body(LAPS * SLOTS + i, LAPS, i)

        def sessions(body):
            def run(eng):
                body(0, 0, 0)
                with eng.Fori(0, (KB - 2) // 2) as j:
                    body(j * 2 + 1, j, 1)
                    body(j * 2 + 2, j + 1, 0)
                body(KB - 1, (KB - 1) // 2, (KB - 1) % 2)
            return run

        def wait(eng, s, count):
            if not (isinstance(count, int) and count <= 0):
                eng.wait_ge(s, count)

        def width(c):
            return min(NC, N - c * NC)

        def score_slot(kap, par, c):
            return (NCH * par + c) % 2, kap * NCH + (NCH * par + c) // 2

        TABLES, TABLES_F = [], []
        for f, dst in enumerate((colT, rowT, valT)):
            for k in range(0, TC, NC // P):
                TABLES.append((dst, k, min(NC, (TC - k) * P)))
                TABLES_F.append(f)
        assert NCH % 2 == 1 and NG % 2 == 1
        block = ctx.enter_context(nc.Block())

        @block.sync
        def _(sp):
            sp.wait_ge(pads_made, 3)
            for f, arr in enumerate((adj_col, adj_row, adj_val)):
                a = arr if f < 2 else arr.bitcast(I32)
                full = (TC - 1) * P * P
                sp.dma_start(tiles_sb[:, f, 0:TC - 1, :], a[0:full].rearrange("(k p e) -> p k e", p=P, e=P)).then_inc(edges_landed[f], 16)
                sp.dma_start(tiles_sb[0:FT, f, TC - 1, :], a[full:FULL * P].rearrange("(p e) -> p e", e=P)).then_inc(edges_landed[f], 16)
                sp.dma_start(tiles_sb[FT:FT + 1, f, TC - 1, 0:REST], a[FULL * P:NNZ].rearrange("(a e) -> a e", a=1)).then_inc(edges_landed[f], 16)
            for i, arr in enumerate((items, inputs, alias)):
                sp.dma_start(ids_i[:, i, :, :], arr.rearrange("(k p) l -> p k l", p=P)).then_inc(ids_landed, 16)
            sp.dma_start(w1_sb[:], w1.rearrange("(a p) d -> p a d", p=P)).then_inc(weights_landed, 16)
            sp.dma_start(w2_sb[:], w2).then_inc(weights_landed, 16)
            sp.dma_start(glu_sb[:, 0, :], glu1_w).then_inc(weights_landed, 16)
            sp.dma_start(glu_sb[:, 1, :], glu2_w).then_inc(weights_landed, 16)
            sp.dma_start(b1_sb[:], glu1_b.rearrange("(p a) -> p a", a=1)).then_inc(weights_landed, 16)
            sp.dma_start(pos_sb, pos_emb).then_inc(weights_landed, 16)

            def landed(rnd):
                def body(c, lap, slot):
                    sp.wait_ge(gathered[slot], (lap + 1) * (16 * TPC) + rnd * (16 * TPC * (LAPS + (slot < CHUNKS_E % SLOTS))))
                    sp.nop(nofuse=True).then_inc(chunks_landed, 1)
                chunks(sp, body)

            landed(0)
            for c in range(CH):
                sp.wait_ge(h_ready, c + 1)
                sp.dma_start(h1_dram[c * CB * BLOCK:(c + 1) * CB * BLOCK, :].rearrange("(j p) d -> p j d", p=P),
                             sumA[:, c * CB:(c + 1) * CB, :]).then_inc(h_stored, 16)
            sp.wait_ge(seq_idx_ready, 1)
            whole = (NB - 1) * P
            sp.dma_start(e_rows[:, 0:whole].rearrange("p (j d) -> p j d", d=D), E[0:whole, :].rearrange("(j p) d -> p j d", p=P))\
                .then_inc(e_landed, 16)
            sp.dma_start(e_rows[0:N - whole, whole:whole + D], E[whole:N, :]).then_inc(e_landed, 16)
            landed(1)
            for c in range(CH):
                sp.wait_ge(g_thirds, c + 1)
                sp.dma_start(graph_dram[c * CB * BLOCK:(c + 1) * CB * BLOCK, :].rearrange("(j p) d -> p j d", p=P),
                             sumA[:, c * CB:(c + 1) * CB, :]).then_inc(g_stored, 16)

            def store(k, kap, par):
                for u in range(PAIRS):
                    cs = [c for c in (2 * u, 2 * u + 1) if c < NCH]
                    for c in cs:
                        bank, before = score_slot(kap, par, c)
                        sp.wait_ge(scores_out[bank], before + 1)
                        sp.nop(nofuse=True)
                    n0, n1 = cs[0] * NC, min(N, (cs[-1] + 1) * NC)
                    sp.dma_start(out[bass.ds(k * P, P), n0:n1], stage[:, u % STAGES, 0:n1 - n0]).then_inc(stored[u % STAGES], 16)
            sessions(store)(sp)
            for i in range(STAGES):
                sp.wait_ge(stored[i], 16 * USES[i] * KB)

        @block.gpsimd
        def _(pool):
            pool.memset(tiles_sb[:, 0, TC - 1, :], 0).then_inc(pads_made, 1)
            pool.memset(tiles_sb[:, 1, TC - 1, :], NOWHERE).then_inc(pads_made, 1)
            pool.memset(tiles_sb[:, 2, TC - 1, :], 0).then_inc(pads_made, 1)
            pool.memset(ident[:], 0.0).then_inc(ident_zero, 1)
            pool.wait_ge(ident_zero, 1)
            pool.affine_select(out=ident[:], in_=ident[:], compare_op=ALU.not_equal, fill=1.0, base=0,
                               pattern=[[-1, P]], channel_multiplier=1).then_inc(ident_made, 1)
            pool.memset(last_one, 0.0).then_inc(ident_zero, 1)
            pool.wait_ge(ident_zero, 2)
            pool.affine_select(out=last_one, in_=last_one, compare_op=ALU.not_equal, fill=1.0, base=-(P - 1),
                               pattern=[[0, P]], channel_multiplier=1).then_inc(last_made, 1)
            pool.iota(chunk_no, pattern=[[1, CHUNKS_E]], base=0, channel_multiplier=0).then_inc(iotas_made, 1)
            pool.iota(stage_no, pattern=[[1, SC * P]], base=0, channel_multiplier=0).then_inc(iotas_made, 1)
            pool.iota(scol_i[:], pattern=[[P, SC]], base=0, channel_multiplier=1).then_inc(iotas_made, 1)
            pool.iota(iota_i, pattern=[[1, BLOCK]], base=0, channel_multiplier=0).then_inc(iotas_made, 1)
            for rnd in range(LAYERS):
                src = E if rnd == 0 else h1_dram
                if rnd == 1:
                    pool.wait_ge(h_stored, 16 * CH)

                def body(c, lap, slot):
                    pool.wait_ge(idx_ready, c + (rnd * CHUNKS_E + 1))
                    pool.nop(nofuse=True)
                    for t in range(TPC):
                        at = slot * TPC + t
                        pool.indirect_dma_start(ring[:, at * D:(at + 1) * D], None, src[:, :],
                                                bass.IndirectOffsetOnAxis(ap=cur[:, at:at + 1], axis=0)).then_inc(gathered[slot], 16)
                chunks(pool, body)

            pool.wait_ge(g_stored, 16 * CH)
            pool.wait_ge(seq_idx_ready, 1)

            def gather(k, kap, par):
                wait(pool, sess_chain, (k - 1) * L)
                pool.tensor_copy(cur_seq[:, par, :], seq_idx[:, bass.ds(k * L, L)]).then_inc(cur_seq_made, 1)
                pool.wait_ge(cur_seq_made, k + 1)
                pool.nop(nofuse=True)
                for l in range(L):
                    pool.indirect_dma_start(seq[:, par, l, :], None, graph_dram[:, :],
                                            bass.IndirectOffsetOnAxis(ap=cur_seq[:, par, l:l + 1], axis=0)).then_inc(seq_landed[par][l // 4], 16)
            sessions(gather)(pool)

        @block.scalar
        def _(act):
            act.wait_ge(iotas_made, 4)
            act.activation(iota_ps, iota_i, ACT.Copy).then_inc(iota_ready, 1)
            for m, (dst, k, w) in enumerate(TABLES):
                if m % 2 == 1:
                    act.wait_ge(tile_T, m + 1)
                    act.activation(dst[:, k * P:k * P + w], ps_tab[:, 1, 0:w], ACT.Copy).then_inc(tile_out[1], 1)
            act.wait_ge(tile_out[0], 2)
            act.wait_ge(tile_out[1], 2)
            for rnd in range(LAYERS):
                if rnd == 0:
                    for c in range(SLOTS):
                        act.activation(cur[:, c * TPC:(c + 1) * TPC], colT[:, c * TPC:(c + 1) * TPC], ACT.Copy).then_inc(idx_ready, 1)
                    act.wait_ge(stage_tables, 1)

                def body(c, lap, slot):
                    free = act.value_load(free_at[0:1, bass.ds(c, 1)], min_val=0, max_val=STEPS)
                    act.wait_ge(steps_done, free + (rnd * STEPS + DONE0))
                    act.activation(cur[:, slot * TPC:(slot + 1) * TPC], colT[:, bass.ds(c * TPC, TPC)], ACT.Copy).then_inc(idx_ready, 1)

                if rnd == 0:
                    with act.Fori(1, LAPS) as lap:
                        for i in range(SLOTS):
                            body(lap * SLOTS + i, lap, i)
                    for i in range(CHUNKS_E - LAPS * SLOTS):
                        body(LAPS * SLOTS + i, LAPS, i)
                else:
                    chunks(act, body)
                for c in range(CH):
                    src = (sumA, sumB)[rnd]
                    if c == 0:
                        act.wait_ge(added, ADD0 + (rnd + 1) * STEPS)
                    if c >= 2:
                        act.wait_ge(ssq_made, rnd * CH + c - 1)
                    w = CB * BLOCK
                    act.activation(sq[:, (c % 2) * w:(c % 2 + 1) * w], src[:, c * CB:(c + 1) * CB, :].rearrange("p b f -> p (b f)"),
                                   ACT.Square).then_inc(squared, 1)
                act.wait_ge(ssq_made, (rnd + 1) * CH)
                act.activation(nrm[:], ssq[:], ACT.Sqrt).then_inc(nrm_made, 1)
            for c in range(CH):
                act.wait_ge(h_ready, CH + c + 1)
                v = sumA[:, c * CB:(c + 1) * CB, :].rearrange("p b f -> p (b f)")
                act.activation(v, v, ACT.Copy, scale=1.0 / (LAYERS + 1)).then_inc(g_thirds, 1)
            for c in range(CH):
                act.wait_ge(g_thirds, c + 1)
                v = sumA[:, c * CB:(c + 1) * CB, :].rearrange("p b f -> p (b f)")
                act.activation(sumB[:, c * CB:(c + 1) * CB, :].rearrange("p b f -> p (b f)"), v, ACT.Square).then_inc(graph_sq, 1)
            act.wait_ge(graph_ssq, CH)
            act.activation(nrm[:], ssq[:], ACT.Sqrt).then_inc(graph_nrm, 1)
            for q in range(1, NCH, 2):
                act.wait_ge(graph_T, q + 1)
                w = min(4, NB - 4 * q) * P
                act.activation(graphT[:, q * NC:q * NC + w], ps_big[:, q % 4, 0:w], ACT.Copy).then_inc(graph_out[1], 1)

            def evacuate(k, kap, par, c):
                bank, before = score_slot(kap, par, c)
                if bank == 1:
                    act.wait_ge(scored, k * NCH + c + 1)
                    u = c // 2
                    wait(act, stored[u % STAGES], (k * USES[u % STAGES] + u // STAGES) * 16)
                    act.activation(stage[:, u % STAGES, c % 2 * NC:c % 2 * NC + width(c)], ps_s[:, 1, 0:width(c)], ACT.Copy)\
                        .then_inc(scores_out[1], 1)

            def root(k):
                act.wait_ge(sess_ssq, k + 1)
                act.activation(sess_n[:, 1:2], sess_n[:, 0:1], ACT.Sqrt).then_inc(sess_nrm, 1)

            def batch(k, kap, par):
                first = isinstance(k, int) and k == 0
                for g in range(NG):
                    n = k * NG + g
                    act.wait_ge(w_ready, n + 1)
                    wait(act, g_ready, n - NG + 1)
                    for j in range(GS[g]):
                        l = 4 * g + j
                        t = act.activation(nh[:, l * P:(l + 1) * P], ps_w[:, j * P:(j + 1) * P], ACT.Tanh,
                                           bias=posW[:, L - 1 - l:L - l])
                    t.then_inc(tanh_done, 1)
                    if not first:
                        if g == 3:
                            root(k - 1)
                        for c in CHUNKS[g]:
                            evacuate(k - 1, kap if par else kap - 1, 1 - par, c)
                for g in range(NG):
                    n = k * NG + g
                    act.wait_ge(z_made, n + 1)
                    wait(act, beta_ready, n - 1)
                    w = GS[g] * P
                    act.activation(gate[:, (par + g) % 2, 0:w], z[:, (par + g) % 2, 0:w], ACT.Sigmoid).then_inc(gate_made, 1)

            act.wait_ge(graph_T, NCH)
            sessions(batch)(act)
            root(KB - 1)
            for c in range(NCH):
                evacuate(KB - 1, (KB - 1) // 2, (KB - 1) % 2, c)

        @block.tensor
        def _(pe):
            pe.wait_ge(ident_made, 1)
            for m, (dst, k, w) in enumerate(TABLES):
                f = TABLES_F[m]
                pe.wait_ge(tile_f, f + 1)
                if m >= 2:
                    pe.wait_ge(tile_out[m % 2], m // 2)
                for i in range(w // P):
                    t = pe.transpose(ps_tab[:, m % 2, i * P:(i + 1) * P], tiles_sb[:, f, k + i, :].bitcast(F32), ident[:])
                t.then_inc(tile_T, 1)
            pe.wait_ge(last_made, 1)
            for i in range(2):
                pe.wait_ge(tile_out[i], len(TABLES[i::2]))
            pe.matmul(ps_big[:, 0, 0:CHUNKS_E], last_one, rowT[:, TPC - 1:CHUNKS_E * TPC:TPC], start=True, stop=True).then_inc(last_rows, 1)
            for k in range(SC):
                pe.wait_ge(spread_made, k + 1)
                t = pe.matmul(ps_big[:, 1, k * P:(k + 1) * P], spread[:, k, :], ident[:], start=True, stop=True)
            t.then_inc(blocks_ready, 1)
            pe.wait_ge(weights_landed, 16 * 6)
            pe.transpose(ps_misc[:, 0:L], pos_sb, ident[0:L, 0:L])
            for i in range(2):
                t = pe.transpose(ps_misc[:, 64 + i * P:64 + (i + 1) * P], glu_sb[:, i, :], ident[:])
            t.then_inc(weights_T, 1)
            pe.wait_ge(weights_out, 1)
            pe.matmul(ps_misc[:, 0:L], w1_sb[:, 0, :], posT[:], start=True, stop=True).then_inc(pos_product, 1)
            pe.wait_ge(stage_tables, 1)
            for rnd in range(LAYERS):
                with pe.Fori(0, LOOPS) as r:
                    for i in range(UNROLL):
                        s = r * UNROLL + i
                        at = pe.value_load(slot_at[0:1, bass.ds(s, 1)], min_val=0, max_val=(SLOTS - 1) * TPC * D)
                        need = pe.value_load(need_of[0:1, bass.ds(s, 1)], min_val=1, max_val=CHUNKS_E)
                        pe.wait_ge(onehot_made, s + (rnd * (STEPS + 1) + 1))
                        pe.wait_ge(chunks_landed, need + rnd * CHUNKS_E)
                        pe.wait_ge(added, s + (rnd * STEPS + 1))
                        for t in range(TPC):
                            mm = pe.matmul(ps_big[:, i % BANKS, 0:D], onehot[:, i % 2, t, :], ring[:, bass.ds(at + t * D, D)],
                                           start=(t == 0), stop=(t == TPC - 1))
                        mm.then_inc(steps_done, 1)

            pe.wait_ge(g_stored, 16 * CH)
            for q in range(NCH):
                if q >= 4:
                    pe.wait_ge(graph_out[q % 2], q // 2 - 1)
                for i in range(min(4, NB - 4 * q)):
                    j = 4 * q + i
                    if j % (CB) == 0:
                        pe.wait_ge(graph_unit, j // (CB) + 1)
                    t = pe.transpose(ps_big[:, q % 4, i * P:(i + 1) * P], sumB[:, j, :], ident[:])
                t.then_inc(graph_T, 1)
            pe.wait_ge(graph_out[0], -(-NCH // 2))
            pe.wait_ge(graph_out[1], NCH // 2)

            def turn(k, kap, par, g):
                n = k * NG + g
                pe.wait_ge(seq_landed[par][g], (kap + 1) * (GS[g] * 16))
                wait(pe, x_copied, n - 1)
                for j in range(GS[g]):
                    t = pe.transpose(ps_x[:, (par + g) % 2, j * P:(j + 1) * P], seq[:, par, 4 * g + j, :], ident[:])
                t.then_inc(x_ready, 1)

            def product(k, par, g):
                n = k * NG + g
                pe.wait_ge(x_copied, n + 1)
                wait(pe, tanh_done, n)
                w = GS[g] * P
                pe.matmul(ps_w[:, 0:w], w1_sb[:, 1, :], xT[:, (par + g) % 2, 0:w], start=True, stop=True).then_inc(w_ready, 1)

            def gates(k, par, g):
                n = k * NG + g
                pe.wait_ge(tanh_done, n + 1)
                wait(pe, z_made, n - 1)
                w = GS[g] * P
                pe.matmul(ps_g[:, (par + g) % 2, 0:w], gluT[:, 0, :], nh[:, 4 * g * P:4 * g * P + w], start=True, stop=True)\
                    .then_inc(g_ready, 1)

            def weigh(k, par, g):
                pe.wait_ge(gate_made, k * NG + g + 1)
                for j in range(GS[g]):
                    l = 4 * g + j
                    t = pe.matmul(beta_ps[:, l:l + 1], gate[:, (par + g) % 2, j * P:(j + 1) * P], w2_sb[:], start=True, stop=True)
                t.then_inc(beta_ready, 1)

            def turn_sel(k):
                pe.wait_ge(sel_ready, k + 1)
                pe.transpose(selT_ps, sel, ident[:]).then_inc(selT_ready, 1)

            def score(k, kap, par, c):
                if c == 0:
                    pe.wait_ge(selT_copied, k + 1)
                bank, before = score_slot(kap, par, c)
                wait(pe, scores_out[bank], before)
                pe.matmul(ps_s[:, bank, 0:width(c)], selT, graphT[:, c * NC:c * NC + width(c)], start=True, stop=True)\
                    .then_inc(scored, 1)

            def batch(k, kap, par):
                first = isinstance(k, int) and k == 0
                turn(k, kap, par, 0)
                for g in range(NG):
                    if g + 1 < NG:
                        turn(k, kap, par, g + 1)
                    product(k, par, g)
                    if not first:
                        if g == 4:
                            turn_sel(k - 1)
                        for c in CHUNKS[g]:
                            score(k - 1, kap if par else kap - 1, 1 - par, c)
                pe.wait_ge(hs_ready, k + 1)
                pe.transpose(hsT_ps, hs, ident[:]).then_inc(hsT_ready, 1)
                pe.wait_ge(hsT_copied, k + 1)
                pe.matmul(hg_ps, gluT[:, 1, :], hsT, start=True, stop=True).then_inc(hg_ready, 1)
                gates(k, par, 0)
                for g in range(NG):
                    if g + 1 < NG:
                        gates(k, par, g + 1)
                    weigh(k, par, g)

            sessions(batch)(pe)
            turn_sel(KB - 1)
            for c in range(NCH):
                score(KB - 1, (KB - 1) // 2, (KB - 1) % 2, c)

        @block.vector
        def _(dve):
            links = [0]

            def link(ins):
                links[0] += 1
                ins.then_inc(prep, 1)
                dve.wait_ge(prep, links[0])

            for f in range(2):
                dve.wait_ge(edges_landed[f], 48)
                dve.tensor_copy(tiles_sb[:, f, :, :].bitcast(F32), tiles_sb[:, f, :, :]).then_inc(tile_f, 1)
            dve.wait_ge(edges_landed[2], 48)
            dve.memset(pick, 0.0).then_inc(tile_f, 1)
            for m, (dst, k, w) in enumerate(TABLES):
                if m % 2 == 0:
                    dve.wait_ge(tile_T, m + 1)
                    dve.tensor_copy(dst[:, k * P:k * P + w], ps_tab[:, 0, 0:w]).then_inc(tile_out[0], 1)
            dve.wait_ge(last_rows, 1)
            link(dve.tensor_copy(key_i, ps_big[:, 0, 0:CHUNKS_E]))
            link(dve.tensor_scalar(key_i, key_i, BLOCK.bit_length() - 1, None, ALU.arith_shift_right))
            link(dve.memset(key_i[:, CHUNKS_E - 1:CHUNKS_E], NB - 1))
            dve.wait_ge(iotas_made, 4)
            link(dve.tensor_tensor(key, key_i, chunk_no, ALU.add))
            link(dve.memset(free_at[:], 0))
            link(dve.tensor_scalar(free_at[:, SLOTS:], key[0:1, :], 1.0, None, ALU.add))
            link(dve.tensor_copy(scol[:], scol_i[:]))
            for k in range(SC):
                link(dve.tensor_scalar(junk, key, scol[:, k:k + 1], 0.0, ALU.is_lt, ALU.add, accum_out=ccol[:, k:k + 1]))
            link(dve.tensor_tensor(bcol[:], scol[:], ccol[:], ALU.subtract))
            link(dve.memset(spread, 1.0))
            for k in range(SC):
                dve.tensor_scalar(spread[:, k, :], spread[:, k, :], bcol[:, k:k + 1], None, ALU.mult).then_inc(spread_made, 1)
            dve.wait_ge(blocks_ready, 1)
            row = ps_big[0:1, 1, 0:SC * P]
            link(dve.tensor_scalar(first_row, ps_big[:, 1, 0:SC * P], float(BLOCK), None, ALU.mult))
            link(dve.tensor_scalar(sum_at, row, float(BLOCK), None, ALU.mult))
            link(dve.tensor_tensor(chunk_i, stage_no[0:1, :], row, ALU.subtract))
            link(dve.tensor_scalar(need_of, chunk_i, 1.0, None, ALU.add))
            link(dve.tensor_scalar(col_at, chunk_i, float(TPC), None, ALU.mult))
            link(dve.tensor_scalar(chunk_i, chunk_i, SLOTS - 1, None, ALU.bitwise_and))
            link(dve.tensor_scalar(slot_at, chunk_i, float(TPC * D), None, ALU.mult))
            dve.memset(beta[:, 0:1], 0.0).then_inc(stage_tables, 1)
            dve.wait_ge(tile_out[1], len(TABLES[1::2]))
            dve.wait_ge(iota_ready, 1)
            dve.wait_ge(weights_T, 1)
            dve.tensor_copy(posT[:], ps_misc[:, 0:L])
            dve.tensor_copy(gluT[:].rearrange("p a d -> p (a d)"), ps_misc[:, 64:64 + 2 * P]).then_inc(weights_out, 1)
            dve.wait_ge(pos_product, 1)
            dve.tensor_copy(posW[:], ps_misc[:, 0:L]).then_inc(pos_out, 1)
            link(dve.memset(sumB[:], 0.0))
            dve.memset(sumA[:], 0.0).then_inc(added, ADD0)
            dve.wait_ge(ids_landed, 48)
            link(dve.tensor_scalar(items_f[:], ids_i[:, 0, :, :], float(N - 1), 0.0, ALU.min, ALU.max))
            link(dve.tensor_scalar(mask[:], ids_i[:, 1, :, :].rearrange("p k l -> p (k l)"), 0.0, None, ALU.not_equal))
            link(dve.tensor_reduce(rcnt[:], mask[:].rearrange("p (k l) -> p k l", l=L), AX_X, ALU.add))
            link(dve.reciprocal(rcnt[:], rcnt[:]))
            link(dve.tensor_copy(alias_f[:], ids_i[:, 2, :, :].rearrange("p k l -> p (k l)")))
            link(dve.tensor_copy(iota50, iota_i[:, 0:L]))
            dve.memset(beta[:, 1:2], 0.0).then_inc(steps_done, DONE0)

            def pick_items(l):
                for k in range(KB):
                    dve.wait_ge(picked, l * KB + k)
                    at = k * L + l
                    dve.scalar_tensor_tensor(out=pick, in0=iota50, scalar=alias_f[:, bass.ds(at, 1)], in1=items_f[:, k, :],
                                             op0=ALU.is_equal, op1=ALU.mult, accum_out=seq_idx_f[:, bass.ds(at, 1)]).then_inc(picked, 1)

            for rnd in range(LAYERS):
                acc = (sumA, sumB)[rnd]
                accf = acc[:].rearrange("p b f -> p (b f)")

                def make_onehot(s, i):
                    col = dve.value_load(col_at[0:1, bass.ds(s, 1)], min_val=0, max_val=CHUNKS_E * TPC)
                    dve.wait_ge(steps_done, s + (rnd * STEPS + 1 + DONE0 - 2))
                    dve.tensor_scalar(rel[:, i % 2, :], rowT[:, bass.ds(col, TPC)], first_row[:, bass.ds(s, 1)], None,
                                      ALU.subtract).then_inc(rel_made, 1)
                    dve.wait_ge(rel_made, s + (rnd * (STEPS + 1) + 1))
                    for t in range(TPC):
                        ins = dve.tensor_scalar(onehot[:, i % 2, t, :], iota_ps, rel[:, i % 2, t:t + 1], valT[:, bass.ds(col + t, 1)],
                                                ALU.is_equal, ALU.mult)
                    ins.then_inc(onehot_made, 1)

                def body(r, extra):
                    for i in range(UNROLL):
                        s = r * UNROLL + i
                        make_onehot(s + 1, i + 1)
                        b = dve.value_load(sum_at[0:1, bass.ds(s, 1)], min_val=0, max_val=(NB - 1) * BLOCK)
                        dve.wait_ge(steps_done, s + (rnd * STEPS + 1 + DONE0))
                        dve.wait_ge(added, s + (rnd * STEPS + ADD0))
                        dst = accf[:, bass.ds(b, BLOCK)]
                        dve.tensor_tensor(dst, dst, ps_big[:, i % BANKS, 0:D], ALU.add).then_inc(added, 1)
                    extra(r)

                def nothing(r):
                    pass

                def add_e(r):
                    dve.wait_ge(e_landed, 32)
                    at = (r - (LOOPS - NB // 2)) * (2 * D)
                    dst = sumA[:].rearrange("p b f -> p (b f)")[:, bass.ds(at, 2 * D)]
                    dve.tensor_tensor(dst, dst, e_rows[:, bass.ds(at, 2 * D)], ALU.add).then_inc(added_e, 1)

                make_onehot(0, 0)
                if rnd == 0:
                    with dve.Fori(0, L) as r:
                        body(r, pick_items)
                    with dve.Fori(L, LOOPS) as r:
                        body(r, nothing)
                    dve.wait_ge(picked, KB * L)
                    dve.tensor_copy(seq_idx[:], seq_idx_f[:]).then_inc(seq_idx_ready, 1)
                else:
                    with dve.Fori(0, LOOPS - NB // 2) as r:
                        body(r, nothing)
                    with dve.Fori(LOOPS - NB // 2, LOOPS) as r:
                        body(r, add_e)
                    dve.wait_ge(added_e, NB // 2)
                for c in range(CH):
                    w = CB * BLOCK
                    dve.wait_ge(squared, rnd * CH + c + 1)
                    dve.tensor_reduce(ssq[:, c * CB:(c + 1) * CB],
                                      sq[:, (c % 2) * w:(c % 2 + 1) * w].rearrange("p (j d) -> p j d", d=D), AX_X, ALU.add).then_inc(ssq_made, 1)
                dve.wait_ge(nrm_made, rnd + 1)
                dve.tensor_scalar(nrm[:], nrm[:], EPS, None, ALU.max).then_inc(tail_v, 1)
                dve.wait_ge(tail_v, 2 * rnd + 1)
                dve.reciprocal(inv[:], nrm[:]).then_inc(tail_v, 1)
                dve.wait_ge(tail_v, 2 * rnd + 2)
                for j in range(NB):
                    src = acc[:, j, :]
                    if rnd == 0:
                        ins = dve.tensor_scalar(src, src, inv[:, j:j + 1], None, ALU.mult)
                    else:
                        dst = sumA[:, j, :]
                        ins = dve.scalar_tensor_tensor(out=dst, in0=src, scalar=inv[:, j:j + 1], in1=dst, op0=ALU.mult, op1=ALU.add)
                    if (j + 1) % (CB) == 0:
                        ins.then_inc(h_ready, 1)

            for c in range(CH):
                w = CB * BLOCK
                dve.wait_ge(graph_sq, c + 1)
                dve.tensor_reduce(ssq[:, c * CB:(c + 1) * CB],
                                  sumB[:, c * CB:(c + 1) * CB, :], AX_X, ALU.add).then_inc(graph_ssq, 1)
            dve.wait_ge(graph_nrm, 1)
            dve.tensor_scalar(nrm[:], nrm[:], EPS, None, ALU.max).then_inc(tail_v, 1)
            dve.wait_ge(tail_v, 2 * LAYERS + 1)
            dve.reciprocal(inv[:], nrm[:]).then_inc(tail_v, 1)
            dve.wait_ge(tail_v, 2 * LAYERS + 2)
            for j in range(NB):
                ins = dve.tensor_scalar(sumB[:, j, :], sumA[:, j, :], inv[:, j:j + 1], None, ALU.mult)
                if (j + 1) % (CB) == 0:
                    ins.then_inc(graph_unit, 1)
            for q in range(0, NCH, 2):
                dve.wait_ge(graph_T, q + 1)
                w = min(4, NB - 4 * q) * P
                dve.tensor_copy(graphT[:, q * NC:q * NC + w], ps_big[:, q % 4, 0:w]).then_inc(graph_out[0], 1)

            def turned(k, par, g):
                n = k * NG + g
                dve.wait_ge(x_ready, n + 1)
                wait(dve, w_ready, n - 1)
                w = GS[g] * P
                dve.tensor_copy(xT[:, (par + g) % 2, 0:w], ps_x[:, (par + g) % 2, 0:w]).then_inc(x_copied, 1)

            def mean(k, kap, par, g):
                dve.wait_ge(seq_landed[par][g], (kap + 1) * (GS[g] * 16))
                for l in range(4 * g, 4 * g + GS[g]):
                    m = mask[:, bass.ds(k * L + l, 1)]
                    if l == 0:
                        wait(dve, hsT_ready, k)
                        t = dve.tensor_scalar(hs, seq[:, par, l, :], m, None, ALU.mult)
                    else:
                        dve.wait_ge(hs_chain, k * L + l)
                        t = dve.scalar_tensor_tensor(out=hs, in0=seq[:, par, l, :], scalar=m, in1=hs, op0=ALU.mult, op1=ALU.add)
                    t.then_inc(hs_chain, 1)

            def summed(k, par, l0, l1):
                if l0 == 0:
                    dve.wait_ge(beta_ready, (k + 1) * NG)
                    wait(dve, sess_chain, k * L)
                    dve.tensor_tensor(beta[:], beta_ps, mask[:, bass.ds(k * L, L)], ALU.mult).then_inc(beta_copied, 1)
                    dve.wait_ge(beta_copied, k + 1)
                for l in range(l0, l1):
                    if l == 0:
                        wait(dve, sel_ready, k)
                        t = dve.tensor_scalar(sess, seq[:, par, l, :], beta[:, l:l + 1], None, ALU.mult)
                    else:
                        dve.wait_ge(sess_chain, k * L + l)
                        t = dve.scalar_tensor_tensor(out=sess, in0=seq[:, par, l, :], scalar=beta[:, l:l + 1], in1=sess,
                                                     op0=ALU.mult, op1=ALU.add)
                    t.then_inc(sess_chain, 1)
                if l1 == L:
                    dve.wait_ge(sess_chain, (k + 1) * L)
                    dve.scalar_tensor_tensor(out=sess_sq, in0=sess, scalar=1.0, in1=sess, op0=ALU.mult, op1=ALU.mult,
                                             accum_out=sess_n[:, 0:1]).then_inc(sess_ssq, 1)

            def select(k):
                dve.wait_ge(sess_nrm, k + 1)
                dve.tensor_scalar(sess_n[:, 2:3], sess_n[:, 1:2], EPS, None, ALU.max).then_inc(sel_chain, 1)
                dve.wait_ge(sel_chain, k * 2 + 1)
                dve.reciprocal(sess_n[:, 3:4], sess_n[:, 2:3]).then_inc(sel_chain, 1)
                dve.wait_ge(sel_chain, k * 2 + 2)
                wait(dve, selT_ready, k)
                dve.tensor_scalar(sel, sess, sess_n[:, 3:4], W_K, ALU.mult, ALU.mult).then_inc(sel_ready, 1)

            def selected(k):
                dve.wait_ge(selT_ready, k + 1)
                wait(dve, scored, k * NCH)
                dve.tensor_copy(selT, selT_ps).then_inc(selT_copied, 1)

            def evacuate(k, kap, par, c):
                bank, before = score_slot(kap, par, c)
                if bank == 0:
                    dve.wait_ge(scored, k * NCH + c + 1)
                    u = c // 2
                    wait(dve, stored[u % STAGES], (k * USES[u % STAGES] + u // STAGES) * 16)
                    dve.tensor_copy(stage[:, u % STAGES, c % 2 * NC:c % 2 * NC + width(c)], ps_s[:, 0, 0:width(c)])\
                        .then_inc(scores_out[0], 1)

            THIRD = -(-L // 3)

            def batch(k, kap, par):
                first = isinstance(k, int) and k == 0
                turned(k, par, 0)
                for g in range(NG):
                    if g + 1 < NG:
                        turned(k, par, g + 1)
                    mean(k, kap, par, g)
                    if not first:
                        if g < 3:
                            summed(k - 1, 1 - par, g * THIRD, min(L, (g + 1) * THIRD))
                        if g == 3:
                            select(k - 1)
                        if g == 4:
                            selected(k - 1)
                        for c in CHUNKS[g]:
                            evacuate(k - 1, kap if par else kap - 1, 1 - par, c)
                dve.wait_ge(hs_chain, (k + 1) * L)
                dve.tensor_scalar(hs, hs, rcnt[:, bass.ds(k, 1)], None, ALU.mult).then_inc(hs_ready, 1)
                dve.wait_ge(hsT_ready, k + 1)
                dve.tensor_copy(hsT, hsT_ps).then_inc(hsT_copied, 1)
                dve.wait_ge(hg_ready, k + 1)
                dve.tensor_scalar(hgT, hg_ps, b1_sb[:], None, ALU.add).then_inc(hg_copied, 1)
                dve.wait_ge(hg_copied, k + 1)
                for g in range(NG):
                    n = k * NG + g
                    w = GS[g] * P
                    dve.wait_ge(g_ready, n + 1)
                    wait(dve, gate_made, n - 1)
                    dve.tensor_tensor(z[:, (par + g) % 2, 0:w].rearrange("p (j b) -> p j b", b=P),
                                      ps_g[:, (par + g) % 2, 0:w].rearrange("p (j b) -> p j b", b=P),
                                      hgT.unsqueeze(1).to_broadcast([P, GS[g], P]), ALU.add).then_inc(z_made, 1)

            dve.wait_ge(graph_out[1], NCH // 2)
            nc.disable_value_cache = True
            sessions(batch)(dve)
            summed(KB - 1, (KB - 1) % 2, 0, L)
            select(KB - 1)
            selected(KB - 1)
            for c in range(NCH):
                evacuate(KB - 1, (KB - 1) // 2, (KB - 1) % 2, c)


_INS = ['r_items', 'r_inputs', 'r_alias_inputs', 'L0_rec_adj_row', 'L0_rec_adj_col', 'L0_rec_adj_val', 'L0_rec_E',
        'L0_rec_pos_emb', 'L0_rec_w1', 'L0_rec_w2', 'L0_rec_glu1_w', 'L0_rec_glu1_b', 'L0_rec_glu2_w']
_OUTS = [((1024, 12500), 'float32')]


def kernel(**inputs):
    import numpy as _np
    import concourse.bacc as _bacc
    from concourse import mybir as _mybir
    from concourse.bass_utils import run_bass_kernel_spmd as _run

    nc = _bacc.Bacc("TRN2", target_bir_lowering=False, num_devices=1)
    arrays, args = {}, []
    for name in _INS:
        a = _np.ascontiguousarray(inputs[name])
        arrays[f"in_{name}_dram"] = a
        args.append(nc.dram_tensor(f"in_{name}_dram", a.shape, _mybir.dt.from_np(a.dtype), kind="ExternalInput").ap())
    for i, (shape, dtype) in enumerate(_OUTS):
        dt = _mybir.dt.from_np(_np.dtype(dtype))
        args.append(nc.dram_tensor(f"out_{i}_dram", shape, dt, kind="ExternalOutput").ap())
    rec_kernel(nc, *args)
    r = _run(nc, [arrays], core_ids=[0])
    return r.results[0]["out_0_dram"]
```

```python
from contextlib import ExitStack

import concourse.bass as bass
from concourse import mybir

ALU = mybir.AluOpType
ACT = mybir.ActivationFunctionType
AX_X = mybir.AxisListType.X
F32 = mybir.dt.float32
I32 = mybir.dt.int32

P = 128
LAYERS = 2
BLOCK = 128
TPC = 4
SLOTS = 8
BANKS = 4
UNROLL = 8
NOWHERE = 1 << 20
STAGES = 4
NC = 512
W_K = 12.0
EPS = 1e-12


def rec_kernel(nc, items, inputs, alias, adj_row, adj_col, adj_val, E, pos_emb, w1, w2, glu1_w, glu1_b, glu2_w, out):
    N, D = E.shape
    B, L = items.shape
    NNZ = adj_row.shape[0]
    FULL = NNZ // P
    REST = NNZ - FULL * P
    CHUNKS_E = -(-NNZ // (P * TPC))
    NB = -(-N // BLOCK)
    NP = NB * BLOCK
    STEPS = CHUNKS_E + NB - 1
    TC = -(-NNZ // (P * P))
    SC = -(-STEPS // P)
    LAPS = CHUNKS_E // SLOTS
    KB = B // P
    GS = [4] * (L // 4) + ([L % 4] if L % 4 else [])
    NG = len(GS)
    NCH = -(-N // NC)
    PAIRS = -(-NCH // 2)
    USES = [len(range(i, PAIRS, STAGES)) for i in range(STAGES)]
    C0 = 1
    SHARE = [0] * C0 + [NCH // (NG - C0) + (i < NCH % (NG - C0)) for i in range(NG - C0)]
    CHUNKS = [list(range(sum(SHARE[:g]), sum(SHARE[:g + 1]))) for g in range(NG)]
    LOOPS = STEPS // UNROLL
    FT = FULL % P
    SHIFT = BLOCK.bit_length() - 1
    assert 0 < REST < P and LOOPS * UNROLL == STEPS and D == P and TC * P >= CHUNKS_E * TPC
    assert FT and UNROLL % BANKS == 0 and UNROLL % 2 == 0 and L <= LOOPS and NB % 2 == 0 and NB // 2 <= LOOPS

    FOLD = NB * BLOCK - 1
    h1_dram = nc.dram_tensor("h1_dram", (NP, D), F32, kind="Internal").ap()
    graph_dram = nc.dram_tensor("graph_dram", (NP, D), F32, kind="Internal").ap()

    with ExitStack() as ctx:
        def sb(name, shape, dt=F32):
            return ctx.enter_context(nc.sbuf_tensor(name, shape, dt))

        def sem(name):
            return ctx.enter_context(nc.semaphore(name))

        def pb(name, shape):
            return ctx.enter_context(nc.psum_tensor(name, shape, F32))

        sumA = sb("sumA", [P, NB, BLOCK])
        sumB = sb("sumB", [P, NB, BLOCK])
        seq = sb("seq", [P, 2, L, D])
        small_area = sb("small_area", [P, max(4 * SC * P, 6 * P)])
        big_area = sb("big_area", [P, max(STAGES * 2 * NC, (SLOTS + 2) * TPC * D)])
        ring = big_area[:, 0:SLOTS * TPC * D]
        onehot = big_area[:, SLOTS * TPC * D:(SLOTS + 2) * TPC * D].rearrange("p (s t f) -> p s t f", s=2, t=TPC)
        stage = big_area[:, 0:STAGES * 2 * NC].rearrange("p (s f) -> p s f", s=STAGES)
        table_area = sb("table_area", [P, max(3 * TC * P, 8 * NC)])
        rowT = table_area[:, 0:TC * P]
        valT = table_area[:, TC * P:2 * TC * P]
        colT = table_area[:, 2 * TC * P:3 * TC * P].bitcast(I32)
        folded = seq[:, 0, :, :].rearrange("p l d -> p (l d)")[:, 0:TC * P].bitcast(I32)
        z = table_area[:, 0:2 * NC].rearrange("p (s f) -> p s f", s=2)
        gate = table_area[:, 2 * NC:4 * NC].rearrange("p (s f) -> p s f", s=2)
        x_sum = table_area[:, 4 * NC:5 * NC]
        sess_sum = table_area[:, 5 * NC:6 * NC].rearrange("p (j d) -> p j d", d=D)
        xT = table_area[:, 6 * NC:8 * NC].rearrange("p (s f) -> p s f", s=2)
        slot_at = small_area[0:1, 1 * SC * P:2 * SC * P].bitcast(I32)
        need_of = small_area[0:1, 2 * SC * P:3 * SC * P].bitcast(I32)
        col_at = small_area[0:1, 3 * SC * P:4 * SC * P].bitcast(I32)
        free_at = sb("free_at", [1, SLOTS + CHUNKS_E], I32)
        first_row = small_area[:, 0:SC * P]
        rel = sb("rel", [P, 2, TPC])
        cur = sb("cur", [P, SLOTS * TPC], I32)
        ident = sb("ident", [P, P])
        scol_i = sb("scol_i", [P, SC], I32)
        scol = sb("scol", [P, SC])
        ccol = sb("ccol", [P, SC])
        bcol = sb("bcol", [P, SC])
        ssq = sb("ssq", [P, NB])
        nrm = sb("nrm", [P, NB])
        inv = sb("inv", [P, NB])
        cur_seq = sb("cur_seq", [P, 2, L], I32)
        rcnt = sb("rcnt", [P, KB])
        w1_sb = sb("w1_sb", [P, 2, D])
        gluT = sb("gluT", [P, 2, D])
        tick = sb("tick", [P, 2])
        w2_row = sb("w2_row", [P, D])
        b1_row = sb("b1_row", [P, D])
        beta = sb("beta", [P, L])
        sess_n = sb("sess_n", [P, 4])
        posT = sb("posT", [P, L])
        posW = sb("posW", [P, L])
        hsT = small_area[:, 0 * P:1 * P]
        hg = small_area[:, 1 * P:2 * P]
        sess = small_area[:, 2 * P:3 * P]
        sess_sq = small_area[:, 3 * P:4 * P]
        sel = small_area[:, 4 * P:5 * P]
        selT = small_area[:, 5 * P:6 * P]
        seq_idx = sb("seq_idx", [P, KB * L], I32)
        sq = seq[:, 0, :, :].rearrange("p l d -> p (l d)")
        tiles_sb = seq[:, 1, :, :].rearrange("p l d -> p (l d)").bitcast(I32)[:, 0:TC * 3 * P].rearrange(
            "p (f k e) -> p f k e", k=TC, f=3)
        e_rows = seq[:].rearrange("p a l d -> p (a l d)")[:, 0:NB * D]
        ids_i = seq[:, 1, :, :].rearrange("p l d -> p (l d)").bitcast(I32)[:, 3 * TC * P:3 * TC * P + 3 * KB * L].rearrange(
            "p (f k l) -> p f k l", f=3, k=KB)
        mask = seq[:, 1, 0:4, :].rearrange("p l d -> p (l d)")[:, 0:KB * L]
        items_f = sq[:, 4740:4740 + KB * L].rearrange("p (k l) -> p k l", k=KB)
        alias_f = sq[:, 5140:5140 + KB * L]
        seq_idx_f = sq[:, 5540:5540 + KB * L]
        pick = sq[:, 5940:5940 + L]
        iota50 = sq[:, 6000:6000 + L]
        glu_sb = sq[:, 4096:4096 + 2 * D].rearrange("p (a d) -> p a d", a=2)
        pos_sb = sq[0:L, 4352:4352 + D]
        last_one = sq[:, 4480:4480 + P]
        iota_i = sq[:, 4608:4608 + BLOCK].bitcast(I32)
        key_i = sq[:, 0:CHUNKS_E].bitcast(I32)
        key = sq[:, 512:512 + CHUNKS_E]
        chunk_no = sq[:, 1024:1024 + CHUNKS_E].bitcast(I32)
        stage_no = sq[:, 1536:1536 + SC * P].bitcast(I32)
        sq_junk = seq[:].rearrange("p a l d -> p (a l d)")[:, (2 * L - 1) * D:2 * L * D]
        junk = sq[:, 2048:2048 + CHUNKS_E]
        spread = sq[:, 2560:2560 + SC * P].rearrange("p (k e) -> p k e", e=P)
        chunk_i = sq[0:1, 3584:3584 + SC * P].bitcast(I32)

        ps_big = pb("ps_big", [P, 4, 512])
        ps_tab = pb("ps_tab", [P, 2, 512])
        ps_iota = pb("ps_iota", [P, 512])
        ps_misc = pb("ps_misc", [P, 512])
        ps_x = ps_tab
        ps_w = ps_iota
        ps_g = ps_big[:, 0:2, :]
        ps_s = ps_big[:, 2:4, :]
        hg_ps = ps_misc[:, 0:P]
        selT_ps = ps_misc[:, P:2 * P]
        graphT = sumA[:].rearrange("p b f -> p (b f)")
        nh = sumB[:].rearrange("p b f -> p (b f)")[:, 0:L * P]

        iota_ps = ps_iota[:, 0:BLOCK]

        pads_made = sem("pads_made")
        edges_landed = [sem(f"edges_landed{f}") for f in range(3)]
        ids_landed = sem("ids_landed")
        e_landed = sem("e_landed")
        iotas_made = sem("iotas_made")
        ident_zero = sem("ident_zero")
        ident_made = sem("ident_made")
        last_made = sem("last_made")
        prep = sem("prep")
        tile_f = sem("tile_f")
        tile_T = sem("tile_T")
        tile_out = [sem("tile_out_v"), sem("tile_out_a")]
        last_rows = sem("last_rows")
        spread_made = sem("spread_made")
        blocks_ready = sem("blocks_ready")
        stage_tables = sem("stage_tables")
        iota_ready = sem("iota_ready")
        idx_ready = sem("idx_ready")
        gathered = [sem(f"gathered{i}") for i in range(SLOTS)]
        chunks_landed = sem("chunks_landed")
        onehot_made = sem("onehot_made")
        steps_done = sem("steps_done")
        added = sem("added")
        picked = sem("picked")
        rel_made = sem("rel_made")
        added_e = sem("added_e")
        squared = sem("squared")
        nrm_made = sem("nrm_made")
        tail_v = sem("tail_v")
        inv_made = sem("inv_made")
        rows_ready = [sem("rows_ready_v"), sem("rows_ready_a"), sem("rows_ready_p")]
        scaled = sem("scaled")
        sumA_zero = sem("sumA_zero")
        zeroed = sem("zeroed")
        h_stored = sem("h_stored")
        g_stored = sem("g_stored")
        seq_idx_ready = sem("seq_idx_ready")

        weights_landed = sem("weights_landed")
        weights_T = sem("weights_T")
        weights_out = sem("weights_out")
        pos_product = sem("pos_product")
        graph_sq = sem("graph_sq")
        graph_ssq = sem("graph_ssq")
        graph_nrm = sem("graph_nrm")
        graph_unit = sem("graph_unit")
        graph_T = sem("graph_T")
        graph_out = [sem("graph_out0"), sem("graph_out1")]
        cur_seq_made = sem("cur_seq_made")
        seq_landed = [[sem(f"seq_landed{p}_{g}") for g in range(-(-L // 4))] for p in range(2)]
        x_ready = sem("x_ready")
        x_copied = sem("x_copied")
        x_added = sem("x_added")
        w_ready = sem("w_ready")
        tanh_done = sem("tanh_done")
        hs_ready = sem("hs_ready")
        hg_ready = sem("hg_ready")
        hg_copied = sem("hg_copied")
        g_ready = sem("g_ready")
        z_made = sem("z_made")
        gate_made = sem("gate_made")
        beta_made = sem("beta_made")
        sess_added = sem("sess_added")
        sess_made = sem("sess_made")
        sess_ssq = sem("sess_ssq")
        sess_nrm = sem("sess_nrm")
        sel_chain = sem("sel_chain")
        sel_ready = sem("sel_ready")
        selT_ready = sem("selT_ready")
        selT_copied = sem("selT_copied")
        e_pad = sem("e_pad")
        folded_made = sem("folded_made")
        cols_folded = sem("cols_folded")
        scored = sem("scored")
        scores_out = [sem("scores_out0"), sem("scores_out1")]
        stored = [sem(f"stored{i}") for i in range(STAGES)]

        DONE0 = 2
        ADD0 = BANKS
        CH = 14
        CB = NB // CH
        assert CB * CH == NB and LOOPS <= L + CH
        HELPED = [c % 3 == 1 for c in range(CH)]

        def piece(rows, c):
            return rows[:, c * CB:(c + 1) * CB, :]

        def piece_flat(rows, c):
            return piece(rows, c).rearrange("p b f -> p (b f)")

        def by_partition(rows):
            return rows.rearrange("(p j) d -> p j d", p=P)

        def nth(c):
            return HELPED[:c].count(HELPED[c])

        def chunks(eng, body):
            with eng.Fori(0, LAPS) as lap:
                for i in range(SLOTS):
                    body(lap * SLOTS + i, lap, i)
            for i in range(CHUNKS_E - LAPS * SLOTS):
                body(LAPS * SLOTS + i, LAPS, i)

        def sessions(body):
            def run(eng):
                body(0, 0, 0)
                body(1, 0, 1)
                with eng.Fori(1, KB // 2) as j:
                    body(j * 2, j, 0)
                    body(j * 2 + 1, j, 1)
            return run

        def laps(body):
            def run(eng):
                body(0, 0, 0, (True, False, False))
                body(1, 0, 1, (True, True, False))
                with eng.Fori(1, KB // 2) as j:
                    body(j * 2, j, 0, (True, True, True))
                    body(j * 2 + 1, j, 1, (True, True, True))
                body(KB, KB // 2, 0, (False, True, True))
                body(KB + 1, KB // 2, 1, (False, False, True))
            return run

        def wait(eng, s, count):
            if not (isinstance(count, int) and count <= 0):
                eng.wait_ge(s, count)

        def width(c):
            return min(NC, N - c * NC)

        def score_slot(kap, par, c):
            return (NCH * par + c) % 2, kap * NCH + (NCH * par + c) // 2

        TABLES, TABLES_F = [], []
        for f, dst in enumerate((colT, rowT, valT)):
            for k in range(0, TC, NC // P):
                TABLES.append((dst, k, min(NC, (TC - k) * P)))
                TABLES_F.append(f)
        assert NCH % 2 == 1 and NG % 2 == 1
        block = ctx.enter_context(nc.Block())

        @block.sync
        def _(sp):
            sp.wait_ge(pads_made, 3)
            for f, arr in enumerate((adj_col, adj_row, adj_val)):
                a = arr if f < 2 else arr.bitcast(I32)
                full = (TC - 1) * P * P
                sp.dma_start(tiles_sb[:, f, 0:TC - 1, :], a[0:full].rearrange("(k p e) -> p k e", p=P, e=P)).then_inc(edges_landed[f], 16)
                sp.dma_start(tiles_sb[0:FT, f, TC - 1, :], a[full:FULL * P].rearrange("(p e) -> p e", e=P)).then_inc(edges_landed[f], 16)
                sp.dma_start(tiles_sb[FT:FT + 1, f, TC - 1, 0:REST], a[FULL * P:NNZ].rearrange("(a e) -> a e", a=1)).then_inc(edges_landed[f], 16)
            for i, arr in enumerate((items, inputs, alias)):
                sp.dma_start(ids_i[:, i, :, :], arr.rearrange("(k p) l -> p k l", p=P)).then_inc(ids_landed, 16)
            sp.dma_start(w1_sb[:], w1.rearrange("(a p) d -> p a d", p=P)).then_inc(weights_landed, 16)
            sp.dma_start(w2_row[:], w2.rearrange("d a -> a d").to_broadcast([P, D])).then_inc(weights_landed, 16)
            sp.dma_start(glu_sb[:, 0, :], glu1_w).then_inc(weights_landed, 16)
            sp.dma_start(glu_sb[:, 1, :], glu2_w).then_inc(weights_landed, 16)
            sp.dma_start(b1_row[:], glu1_b.rearrange("(a d) -> a d", a=1).to_broadcast([P, D])).then_inc(weights_landed, 16)
            sp.dma_start(pos_sb, pos_emb).then_inc(weights_landed, 16)

            def landed(rnd):
                def body(c, lap, slot):
                    sp.wait_ge(gathered[slot], (lap + 1) * (16 * TPC) + rnd * (16 * TPC * (LAPS + (slot < CHUNKS_E % SLOTS))))
                    sp.nop(nofuse=True).then_inc(chunks_landed, 1)
                chunks(sp, body)

            landed(0)
            for c in range(CH):
                sp.wait_ge(rows_ready[HELPED[c]], nth(c) + 1)
                sp.dma_start(by_partition(h1_dram)[:, c * CB:(c + 1) * CB, :],
                             sumA[:, c * CB:(c + 1) * CB, :]).then_inc(h_stored, 16)
            sp.wait_ge(e_pad, 1)
            sp.wait_ge(cols_folded, 1)
            whole = (NB - 1) * P
            sp.dma_start(e_rows[:, 0:whole].rearrange("p (j d) -> p j d", d=D), E[0:whole, :].rearrange("(j p) d -> p j d", p=P))\
                .then_inc(e_landed, 16)
            sp.dma_start(e_rows[0:N - whole, whole:whole + D], E[whole:N, :]).then_inc(e_landed, 16)
            landed(1)
            for c in range(CH):
                if HELPED[c]:
                    sp.wait_ge(rows_ready[2], nth(c) + 1)
                else:
                    sp.wait_ge(rows_ready[0], HELPED.count(False) + nth(c) + 1)
                sp.dma_start(by_partition(graph_dram)[:, c * CB:(c + 1) * CB, :],
                             sumA[:, c * CB:(c + 1) * CB, :]).then_inc(g_stored, 16)

            def store(k, kap, par):
                for u in range(PAIRS):
                    cs = [c for c in (2 * u, 2 * u + 1) if c < NCH]
                    for c in cs:
                        bank, before = score_slot(kap, par, c)
                        sp.wait_ge(scores_out[bank], before + 2)
                        sp.nop(nofuse=True)
                    n0, n1 = cs[0] * NC, min(N, (cs[-1] + 1) * NC)
                    sp.dma_start(out[bass.ds(k * P, P), n0:n1], stage[:, u % STAGES, 0:n1 - n0]).then_inc(stored[u % STAGES], 16)
            for i in range(STAGES):
                sp.nop(nofuse=True).then_inc(stored[i], 16)
            sessions(store)(sp)
            for i in range(STAGES):
                sp.wait_ge(stored[i], 16 * USES[i] * KB + 16)

        @block.gpsimd
        def _(pool):
            pool.memset(tiles_sb[:, 0, TC - 1, :], 0).then_inc(pads_made, 1)
            pool.memset(tiles_sb[:, 1, TC - 1, :], NOWHERE).then_inc(pads_made, 1)
            pool.memset(tiles_sb[:, 2, TC - 1, :], 0).then_inc(pads_made, 1)
            pool.memset(ident[:], 0.0).then_inc(ident_zero, 1)
            pool.wait_ge(ident_zero, 1)
            pool.affine_select(out=ident[:], in_=ident[:], compare_op=ALU.not_equal, fill=1.0, base=0,
                               pattern=[[-1, P]], channel_multiplier=1).then_inc(ident_made, 1)
            pool.memset(last_one, 0.0).then_inc(ident_zero, 1)
            pool.wait_ge(ident_zero, 2)
            pool.affine_select(out=last_one, in_=last_one, compare_op=ALU.not_equal, fill=1.0, base=-(P - 1),
                               pattern=[[0, P]], channel_multiplier=1).then_inc(last_made, 1)
            pool.iota(chunk_no, pattern=[[1, CHUNKS_E]], base=0, channel_multiplier=0).then_inc(iotas_made, 1)
            pool.iota(stage_no, pattern=[[1, SC * P]], base=0, channel_multiplier=0).then_inc(iotas_made, 1)
            pool.iota(scol_i[:], pattern=[[P, SC]], base=0, channel_multiplier=1).then_inc(iotas_made, 1)
            pool.iota(iota_i, pattern=[[1, BLOCK]], base=0, channel_multiplier=0).then_inc(iotas_made, 1)
            pool.memset(sumA[:], 0.0).then_inc(sumA_zero, 1)
            for rnd in range(LAYERS):
                src = E if rnd == 0 else h1_dram
                if rnd == 1:
                    pool.wait_ge(folded_made, 3)
                    pool.wait_ge(idx_ready, CHUNKS_E)
                    pool.tensor_copy(colT, folded).then_inc(cols_folded, 1)
                    pool.wait_ge(h_stored, 16 * CH)

                def body(c, lap, slot):
                    pool.wait_ge(idx_ready, c + (rnd * CHUNKS_E + 1))
                    pool.nop(nofuse=True)
                    for t in range(TPC):
                        at = slot * TPC + t
                        pool.indirect_dma_start(ring[:, at * D:(at + 1) * D], None, src[:, :],
                                                bass.IndirectOffsetOnAxis(ap=cur[:, at:at + 1], axis=0)).then_inc(gathered[slot], 16)
                chunks(pool, body)

            for c in range(CH):
                if HELPED[c]:
                    pool.wait_ge(scaled, nth(c) + 1)
                    pool.tensor_tensor(piece_flat(sumA, c), piece_flat(sumA, c), piece_flat(sumB, c), ALU.add).then_inc(rows_ready[2], 1)

            pool.wait_ge(g_stored, 16 * CH)
            pool.wait_ge(seq_idx_ready, 1)

            def gather(k, kap, par):
                wait(pool, x_ready, (k - 1) * NG)
                pool.tensor_copy(cur_seq[:, par, :], seq_idx[:, bass.ds(k * L, L)]).then_inc(cur_seq_made, 1)
                pool.wait_ge(cur_seq_made, k + 1)
                pool.nop(nofuse=True)
                for g in range(NG):
                    if not (isinstance(k, int) and k < 2):
                        pool.wait_ge(sess_added, (k - 2) * NG + g + 1)
                    pool.nop(nofuse=True)
                    for l in range(4 * g, 4 * g + GS[g]):
                        pool.indirect_dma_start(seq[:, par, l, :], None, graph_dram[:, :],
                                                bass.IndirectOffsetOnAxis(ap=cur_seq[:, par, l:l + 1], axis=0)).then_inc(seq_landed[par][g], 16)
            sessions(gather)(pool)

        @block.scalar
        def _(act):
            act.wait_ge(iotas_made, 4)
            act.activation(iota_ps, iota_i, ACT.Copy).then_inc(iota_ready, 1)
            act.wait_ge(tile_out[0], 1)
            for c in range(SLOTS):
                act.activation(cur[:, c * TPC:(c + 1) * TPC], colT[:, c * TPC:(c + 1) * TPC], ACT.Copy).then_inc(idx_ready, 1)
            for m, (dst, k, w) in enumerate(TABLES):
                if m % 2 == 1:
                    act.wait_ge(tile_T, m + 1)
                    act.activation(dst[:, k * P:k * P + w], ps_tab[:, 1, 0:w], ACT.Copy).then_inc(tile_out[1], 1)
            act.wait_ge(tile_out[0], 2)
            act.wait_ge(tile_out[1], 2)
            for rnd in range(LAYERS):
                if rnd == 0:
                    act.wait_ge(stage_tables, 1)

                def body(c, lap, slot):
                    free = act.value_load(free_at[0:1, bass.ds(c, 1)], min_val=0, max_val=STEPS)
                    act.wait_ge(steps_done, free + (rnd * STEPS + DONE0))
                    act.activation(cur[:, slot * TPC:(slot + 1) * TPC], colT[:, bass.ds(c * TPC, TPC)], ACT.Copy).then_inc(idx_ready, 1)

                if rnd == 0:
                    with act.Fori(1, LAPS) as lap:
                        for i in range(SLOTS):
                            body(lap * SLOTS + i, lap, i)
                    for i in range(CHUNKS_E - LAPS * SLOTS):
                        body(LAPS * SLOTS + i, LAPS, i)
                else:
                    act.wait_ge(cols_folded, 1)
                    chunks(act, body)
                act.wait_ge(squared, (rnd + 1) * STEPS + 1)
                act.activation(nrm[:], ssq[:], ACT.Sqrt).then_inc(nrm_made, 1)
                act.wait_ge(inv_made, rnd + 1)
                acc = (sumA, sumB)[rnd]
                for c in range(CH):
                    if HELPED[c]:
                        for j in range(c * CB, (c + 1) * CB):
                            t = act.activation(acc[:, j, :], acc[:, j, :], ACT.Copy, scale=inv[:, j:j + 1])
                        t.then_inc((rows_ready[1], scaled)[rnd], 1)
            for c in range(CH):
                if HELPED[c]:
                    act.wait_ge(rows_ready[2], nth(c) + 1)
                else:
                    act.wait_ge(rows_ready[0], HELPED.count(False) + nth(c) + 1)
                act.activation(piece_flat(sumB, c), piece_flat(sumA, c), ACT.Square).then_inc(graph_sq, 1)
            act.wait_ge(graph_ssq, CH)
            act.activation(nrm[:], ssq[:], ACT.Sqrt).then_inc(graph_nrm, 1)
            for q in range(1, NCH, 2):
                act.wait_ge(graph_T, q + 1)
                w = min(4, NB - 4 * q) * P
                act.activation(graphT[:, q * NC:q * NC + w], ps_big[:, q % 4, 0:w], ACT.Copy).then_inc(graph_out[1], 1)

            def evacuate(k, kap, par, c):
                bank, before = score_slot(kap, par, c)
                if bank == 1:
                    act.wait_ge(scored, k * NCH + c + 1)
                    u = c // 2
                    act.wait_ge(stored[u % STAGES], (k * USES[u % STAGES] + u // STAGES) * 16 + 16)
                    act.activation(stage[:, u % STAGES, c % 2 * NC:c % 2 * NC + width(c)], ps_s[:, 1, 0:width(c)], ACT.Copy)\
                        .then_inc(scores_out[1], 1)

            def turned(k, par, g):
                n = k * NG + g
                act.wait_ge(x_ready, n + 1)
                if isinstance(k, int):
                    wait(act, x_added, n - 1)
                w = GS[g] * P
                act.activation(xT[:, (par + g) % 2, 0:w], ps_x[:, (par + g) % 2, 0:w], ACT.Copy).then_inc(x_copied, 1)

            def bend(k, g):
                n = k * NG + g
                act.wait_ge(w_ready, n + 1)
                wait(act, g_ready, n - NG + 1)
                for j in range(GS[g]):
                    l = 4 * g + j
                    t = act.activation(nh[:, l * P:(l + 1) * P], ps_w[:, j * P:(j + 1) * P], ACT.Tanh,
                                       bias=posW[:, L - 1 - l:L - l])
                t.then_inc(tanh_done, 1)

            def squash(k, par, g):
                n = k * NG + g
                act.wait_ge(z_made, n + 1)
                w = GS[g] * P
                act.activation(gate[:, (par + g) % 2, 0:w], z[:, (par + g) % 2, 0:w], ACT.Sigmoid).then_inc(gate_made, 1)

            def root(k):
                act.wait_ge(sess_ssq, k + 1)
                act.activation(sess_n[:, 1:2], sess_n[:, 0:1], ACT.Sqrt).then_inc(sess_nrm, 1)

            def lap(k, kap, par, has):
                takes, weighs, scores = has
                if takes:
                    turned(k, par, 0)
                if scores:
                    root(k - 2)
                for g in range(NG):
                    if takes:
                        if g + 1 < NG:
                            turned(k, par, g + 1)
                        bend(k, g)
                    if weighs:
                        squash(k - 1, 1 - par, g)
                    if scores:
                        for c in CHUNKS[g]:
                            evacuate(k - 2, kap - 1, par, c)

            act.wait_ge(graph_T, NCH)
            act.nop(nofuse=True).then_inc(scores_out[1], 1)
            laps(lap)(act)

        @block.tensor
        def _(pe):
            pe.wait_ge(ident_made, 1)
            for m, (dst, k, w) in enumerate(TABLES):
                f = TABLES_F[m]
                pe.wait_ge(tile_f, f + 1)
                if m >= 2:
                    pe.wait_ge(tile_out[m % 2], m // 2)
                for i in range(w // P):
                    t = pe.transpose(ps_tab[:, m % 2, i * P:(i + 1) * P], tiles_sb[:, f, k + i, :].bitcast(F32), ident[:])
                t.then_inc(tile_T, 1)
            pe.wait_ge(last_made, 1)
            for i in range(2):
                pe.wait_ge(tile_out[i], len(TABLES[i::2]))
            pe.matmul(ps_big[:, 0, 0:CHUNKS_E], last_one, rowT[:, TPC - 1:CHUNKS_E * TPC:TPC], start=True, stop=True).then_inc(last_rows, 1)
            for k in range(SC):
                pe.wait_ge(spread_made, k + 1)
                t = pe.matmul(ps_big[:, 1, k * P:(k + 1) * P], spread[:, k, :], ident[:], start=True, stop=True)
            t.then_inc(blocks_ready, 1)
            pe.wait_ge(weights_landed, 16 * 6)
            pe.transpose(ps_misc[:, 0:L], pos_sb, ident[0:L, 0:L])
            for i in range(2):
                t = pe.transpose(ps_misc[:, 64 + i * P:64 + (i + 1) * P], glu_sb[:, i, :], ident[:])
            t.then_inc(weights_T, 1)
            pe.wait_ge(weights_out, 1)
            pe.matmul(ps_misc[:, 0:L], w1_sb[:, 0, :], posT[:], start=True, stop=True).then_inc(pos_product, 1)
            pe.wait_ge(stage_tables, 1)
            for rnd in range(LAYERS):
                with pe.Fori(0, LOOPS) as r:
                    for i in range(UNROLL):
                        s = r * UNROLL + i
                        at = pe.value_load(slot_at[0:1, bass.ds(s, 1)], min_val=0, max_val=(SLOTS - 1) * TPC * D)
                        need = pe.value_load(need_of[0:1, bass.ds(s, 1)], min_val=1, max_val=CHUNKS_E)
                        pe.wait_ge(onehot_made, s + (rnd * (STEPS + 1) + 1))
                        pe.wait_ge(chunks_landed, need + rnd * CHUNKS_E)
                        pe.wait_ge(added, s + (rnd * STEPS + 1))
                        for t in range(TPC):
                            mm = pe.matmul(ps_big[:, i % BANKS, 0:D], onehot[:, i % 2, t, :], ring[:, bass.ds(at + t * D, D)],
                                           start=(t == 0), stop=(t == TPC - 1))
                        mm.then_inc(steps_done, 1)

            pe.wait_ge(g_stored, 16 * CH)
            for q in range(NCH):
                if q >= 4:
                    pe.wait_ge(graph_out[q % 2], q // 2 - 1)
                for i in range(min(4, NB - 4 * q)):
                    j = 4 * q + i
                    if j % (CB) == 0:
                        pe.wait_ge(graph_unit, j // (CB) + 1)
                    t = pe.transpose(ps_big[:, q % 4, i * P:(i + 1) * P], sumB[:, j, :], ident[:])
                t.then_inc(graph_T, 1)
            pe.wait_ge(graph_out[0], -(-NCH // 2))
            pe.wait_ge(graph_out[1], NCH // 2)

            def turn(k, kap, par, g):
                n = k * NG + g
                pe.wait_ge(seq_landed[par][g], (kap + 1) * (GS[g] * 16))
                for j in range(GS[g]):
                    t = pe.transpose(ps_x[:, (par + g) % 2, j * P:(j + 1) * P], seq[:, par, 4 * g + j, :], ident[:])
                t.then_inc(x_ready, 1)

            def product(k, par, g):
                n = k * NG + g
                pe.wait_ge(x_copied, n + 1)
                wait(pe, tanh_done, n)
                w = GS[g] * P
                pe.matmul(ps_w[:, 0:w], w1_sb[:, 1, :], xT[:, (par + g) % 2, 0:w], start=True, stop=True).then_inc(w_ready, 1)

            def hidden(k):
                pe.wait_ge(hs_ready, k + 1)
                pe.matmul(hg_ps, hsT, gluT[:, 1, :], start=True, stop=True).then_inc(hg_ready, 1)

            def gates(k, par, g, takes):
                n = k * NG + g
                if not takes:
                    pe.wait_ge(tanh_done, n + 1)
                wait(pe, z_made, n - 1)
                for j in range(GS[g]):
                    l = 4 * g + j
                    t = pe.matmul(ps_g[:, (par + g) % 2, j * P:(j + 1) * P], nh[:, l * P:(l + 1) * P], gluT[:, 0, :],
                                  start=True, stop=True)
                t.then_inc(g_ready, 1)

            def turn_sel(k, weighs):
                pe.wait_ge(sel_ready, k + 1)
                if weighs:
                    pe.wait_ge(hg_copied, k + 2)
                pe.transpose(selT_ps, sel, ident[:]).then_inc(selT_ready, 1)

            def score(k, kap, par, c):
                if c == 0:
                    pe.wait_ge(selT_copied, k + 1)
                bank, before = score_slot(kap, par, c)
                pe.wait_ge(scores_out[bank], before + 1)
                pe.matmul(ps_s[:, bank, 0:width(c)], selT, graphT[:, c * NC:c * NC + width(c)], start=True, stop=True)\
                    .then_inc(scored, 1)

            def lap(k, kap, par, has):
                takes, weighs, scores = has
                if takes:
                    turn(k, kap, par, 0)
                for g in range(NG):
                    if takes:
                        if g + 1 < NG:
                            turn(k, kap, par, g + 1)
                        product(k, par, g)
                    if weighs:
                        if g == 0:
                            hidden(k - 1)
                        gates(k - 1, 1 - par, g, takes)
                    if scores:
                        if g == 0:
                            turn_sel(k - 2, weighs)
                        for c in CHUNKS[g]:
                            score(k - 2, kap - 1, par, c)

            laps(lap)(pe)

        @block.vector
        def _(dve):
            links = [0]

            def link(ins):
                links[0] += 1
                ins.then_inc(prep, 1)
                dve.wait_ge(prep, links[0])

            for f in range(2):
                dve.wait_ge(edges_landed[f], 48)
                dve.tensor_copy(tiles_sb[:, f, :, :].bitcast(F32), tiles_sb[:, f, :, :]).then_inc(tile_f, 1)
            dve.wait_ge(edges_landed[2], 48)
            dve.memset(pick, 0.0).then_inc(tile_f, 1)
            for m, (dst, k, w) in enumerate(TABLES):
                if m % 2 == 0:
                    dve.wait_ge(tile_T, m + 1)
                    dve.tensor_copy(dst[:, k * P:k * P + w], ps_tab[:, 0, 0:w]).then_inc(tile_out[0], 1)
            dve.wait_ge(last_rows, 1)
            link(dve.tensor_copy(key_i, ps_big[:, 0, 0:CHUNKS_E]))
            link(dve.tensor_scalar(key_i, key_i, SHIFT, None, ALU.arith_shift_right))
            link(dve.memset(key_i[:, CHUNKS_E - 1:CHUNKS_E], NB - 1))
            dve.wait_ge(iotas_made, 4)
            link(dve.tensor_tensor(key, key_i, chunk_no, ALU.add))
            link(dve.memset(free_at[:], 0))
            link(dve.tensor_scalar(free_at[:, SLOTS:], key[0:1, :], 1.0, None, ALU.add))
            link(dve.tensor_copy(scol[:], scol_i[:]))
            for k in range(SC):
                link(dve.tensor_scalar(junk, key, scol[:, k:k + 1], 0.0, ALU.is_lt, ALU.add, accum_out=ccol[:, k:k + 1]))
            link(dve.tensor_tensor(bcol[:], scol[:], ccol[:], ALU.subtract))
            link(dve.memset(spread, 1.0))
            for k in range(SC):
                dve.tensor_scalar(spread[:, k, :], spread[:, k, :], bcol[:, k:k + 1], None, ALU.mult).then_inc(spread_made, 1)
            dve.wait_ge(blocks_ready, 1)
            row = ps_big[0:1, 1, 0:SC * P]
            link(dve.tensor_scalar(first_row, ps_big[:, 1, 0:SC * P], float(BLOCK), None, ALU.mult))
            link(dve.tensor_tensor(chunk_i, stage_no[0:1, :], row, ALU.subtract))
            link(dve.tensor_scalar(need_of, chunk_i, 1.0, None, ALU.add))
            link(dve.tensor_scalar(col_at, chunk_i, float(TPC), None, ALU.mult))
            link(dve.tensor_scalar(chunk_i, chunk_i, SLOTS - 1, None, ALU.bitwise_and))
            link(dve.tensor_scalar(slot_at, chunk_i, float(TPC * D), None, ALU.mult))
            dve.memset(tick[:, 0:1], 0.0).then_inc(stage_tables, 1)
            dve.wait_ge(tile_out[1], len(TABLES[1::2]))
            dve.wait_ge(iota_ready, 1)
            dve.wait_ge(weights_T, 1)
            dve.tensor_copy(posT[:], ps_misc[:, 0:L])
            dve.tensor_copy(gluT[:].rearrange("p a d -> p (a d)"), ps_misc[:, 64:64 + 2 * P]).then_inc(weights_out, 1)
            dve.wait_ge(pos_product, 1)
            dve.tensor_copy(posW[:], ps_misc[:, 0:L])
            dve.wait_ge(sumA_zero, 1)
            dve.memset(tick[:, 0:1], 0.0).then_inc(added, ADD0)
            dve.wait_ge(ids_landed, 48)
            link(dve.tensor_scalar(items_f[:], ids_i[:, 0, :, :], float(N - 1), 0.0, ALU.min, ALU.max))
            link(dve.tensor_scalar(mask, ids_i[:, 1, :, :].rearrange("p k l -> p (k l)"), 0.0, None, ALU.not_equal))
            link(dve.tensor_reduce(rcnt[:], mask.rearrange("p (k l) -> p k l", l=L), AX_X, ALU.add))
            link(dve.reciprocal(rcnt[:], rcnt[:]))
            link(dve.tensor_copy(alias_f[:], ids_i[:, 2, :, :].rearrange("p k l -> p (k l)")))
            dve.tensor_copy(iota50, iota_i[:, 0:L]).then_inc(picked, 1)
            dve.memset(tick[:, 1:2], 0.0).then_inc(squared, 1)
            dve.memset(tick[:, 0:1], 0.0).then_inc(steps_done, DONE0)

            def pick_items(l):
                for k in range(KB):
                    dve.wait_ge(picked, l * KB + k + 1)
                    at = k * L + l
                    dve.scalar_tensor_tensor(out=pick, in0=iota50, scalar=alias_f[:, bass.ds(at, 1)], in1=items_f[:, k, :],
                                             op0=ALU.is_equal, op1=ALU.mult, accum_out=seq_idx_f[:, bass.ds(at, 1)]).then_inc(picked, 1)

            def clear(r):
                rows = sumB[:].rearrange("p b f -> p (b f)")[:, bass.ds((r - (LOOPS - CH)) * (CB * BLOCK), CB * BLOCK)]
                dve.tensor_scalar(rows, rowT[:, 0:CB * BLOCK], 0.0, None, ALU.mult).then_inc(zeroed, 1)

            for rnd in range(LAYERS):
                acc = (sumA, sumB)[rnd]
                accf = acc[:].rearrange("p b f -> p (b f)")

                def square(s, b):
                    dve.wait_ge(added, s + (rnd * STEPS + ADD0 + 1))
                    dve.wait_ge(squared, s + (rnd * STEPS + 1))
                    rows = accf[:, bass.ds(b, BLOCK)]
                    dve.scalar_tensor_tensor(out=sq_junk, in0=rows, scalar=1.0, in1=rows, op0=ALU.mult, op1=ALU.mult,
                                             accum_out=ssq[:, bass.ds(b >> SHIFT, 1)]).then_inc(squared, 1)

                def make_onehot(s, i, between=None):
                    col = dve.value_load(col_at[0:1, bass.ds(s, 1)], min_val=0, max_val=CHUNKS_E * TPC)
                    dve.wait_ge(steps_done, s + (rnd * STEPS + 1 + DONE0 - 2))
                    dve.tensor_scalar(rel[:, i % 2, :], rowT[:, bass.ds(col, TPC)], first_row[:, bass.ds(s, 1)], None,
                                      ALU.subtract).then_inc(rel_made, 1)
                    if between:
                        between()
                    dve.wait_ge(rel_made, s + (rnd * (STEPS + 1) + 1))
                    for t in range(TPC):
                        ins = dve.tensor_scalar(onehot[:, i % 2, t, :], iota_ps, rel[:, i % 2, t:t + 1], valT[:, bass.ds(col + t, 1)],
                                                ALU.is_equal, ALU.mult)
                    ins.then_inc(onehot_made, 1)
                    return col

                def body(r, extra):
                    b = None
                    for i in range(UNROLL):
                        s = r * UNROLL + i
                        before = (lambda s=s - 1, b=b: square(s, b)) if i else None
                        after = make_onehot(s + 1, i + 1, before)
                        if i == 0:
                            col = dve.value_load(col_at[0:1, bass.ds(s, 1)], min_val=0, max_val=CHUNKS_E * TPC)
                        b = (s * BLOCK - col * (BLOCK // TPC)).with_bounds(min_val=0, max_val=(NB - 1) * BLOCK)
                        col = after
                        dve.wait_ge(steps_done, s + (rnd * STEPS + 1 + DONE0))
                        dve.wait_ge(added, s + (rnd * STEPS + ADD0))
                        dve.wait_ge(squared, s + (rnd * STEPS + 1))
                        dst = accf[:, bass.ds(b, BLOCK)]
                        dve.tensor_tensor(dst, dst, ps_big[:, i % BANKS, 0:D], ALU.add).then_inc(added, 1)
                    extra(r)
                    square(s, b)

                def nothing(r):
                    pass

                def add_e(r):
                    dve.wait_ge(e_landed, 32)
                    at = (r - (LOOPS - NB // 2)) * (2 * D)
                    dst = sumA[:].rearrange("p b f -> p (b f)")[:, bass.ds(at, 2 * D)]
                    dve.tensor_tensor(dst, dst, e_rows[:, bass.ds(at, 2 * D)], ALU.add).then_inc(added_e, 1)
                    dve.wait_ge(added_e, (r - (LOOPS - NB // 2)) * 2 + 1)
                    dve.tensor_scalar(dst, dst, 1.0 / (LAYERS + 1), None, ALU.mult).then_inc(added_e, 1)

                make_onehot(0, 0)
                if rnd == 0:
                    dve.tensor_scalar(folded, colT, SHIFT, None, ALU.arith_shift_right).then_inc(folded_made, 1)
                    dve.wait_ge(folded_made, 1)
                    dve.tensor_scalar(folded, folded, float(-FOLD), None, ALU.mult).then_inc(folded_made, 1)
                    dve.wait_ge(folded_made, 2)
                    dve.scalar_tensor_tensor(out=folded, in0=colT, scalar=float(NB), in1=folded,
                                             op0=ALU.mult, op1=ALU.add).then_inc(folded_made, 1)
                    def pick_and_clear(r):
                        pick_items(r)
                        clear(r)

                    with dve.Fori(0, LOOPS - CH) as r:
                        body(r, pick_items)
                    with dve.Fori(LOOPS - CH, L) as r:
                        body(r, pick_and_clear)
                    dve.wait_ge(picked, KB * L + 1)
                    link(dve.tensor_copy(seq_idx[:], seq_idx_f))
                    link(dve.tensor_scalar(seq_idx[:], seq_idx[:], SHIFT, None, ALU.arith_shift_right))
                    link(dve.tensor_scalar(seq_idx_f, seq_idx_f, float(NB), None, ALU.mult))
                    link(dve.scalar_tensor_tensor(out=seq_idx_f, in0=seq_idx[:], scalar=float(-FOLD), in1=seq_idx_f,
                                                  op0=ALU.mult, op1=ALU.add))
                    link(dve.tensor_scalar(seq_idx_f, seq_idx_f, float(1 - NP), None, ALU.add))
                    link(dve.tensor_tensor(seq_idx_f, seq_idx_f, mask, ALU.mult))
                    dve.tensor_scalar(seq_idx[:], seq_idx_f, float(NP - 1), None, ALU.add).then_inc(seq_idx_ready, 1)
                    with dve.Fori(L, LOOPS) as r:
                        body(r, clear)
                    dve.wait_ge(zeroed, CH)
                else:
                    with dve.Fori(0, LOOPS - NB // 2) as r:
                        body(r, nothing)
                    with dve.Fori(LOOPS - NB // 2, LOOPS) as r:
                        body(r, add_e)
                    dve.wait_ge(added_e, NB // 2 * 2)
                if rnd == 0:
                    dve.memset(e_rows[:, (NB - 1) * D:NB * D], 0.0).then_inc(e_pad, 1)
                dve.wait_ge(nrm_made, rnd + 1)
                dve.tensor_scalar(nrm[:], nrm[:], EPS, (1.0, LAYERS + 1.0)[rnd], ALU.max, ALU.mult).then_inc(tail_v, 1)
                dve.wait_ge(tail_v, rnd + 1)
                dve.reciprocal(inv[:], nrm[:]).then_inc(inv_made, 1)
                dve.wait_ge(inv_made, rnd + 1)
                for c in range(CH):
                    if HELPED[c]:
                        continue
                    if rnd == 0:
                        ins = dve.tensor_tensor(piece(acc, c), piece(acc, c),
                                                inv[:, c * CB:(c + 1) * CB].unsqueeze(2).to_broadcast([P, CB, BLOCK]), ALU.mult)
                    else:
                        for j in range(c * CB, (c + 1) * CB):
                            dst = sumA[:, j, :]
                            ins = dve.scalar_tensor_tensor(out=dst, in0=acc[:, j, :], scalar=inv[:, j:j + 1], in1=dst,
                                                           op0=ALU.mult, op1=ALU.add)
                    ins.then_inc(rows_ready[0], 1)

            for c in range(CH):
                w = CB * BLOCK
                dve.wait_ge(graph_sq, c + 1)
                dve.tensor_reduce(ssq[:, c * CB:(c + 1) * CB],
                                  sumB[:, c * CB:(c + 1) * CB, :], AX_X, ALU.add).then_inc(graph_ssq, 1)
            dve.wait_ge(graph_nrm, 1)
            dve.tensor_scalar(nrm[:], nrm[:], EPS, None, ALU.max).then_inc(tail_v, 1)
            dve.wait_ge(tail_v, LAYERS + 1)
            dve.reciprocal(inv[:], nrm[:]).then_inc(tail_v, 1)
            dve.wait_ge(tail_v, LAYERS + 2)
            for j in range(NB):
                ins = dve.tensor_scalar(sumB[:, j, :], sumA[:, j, :], inv[:, j:j + 1], None, ALU.mult)
                if (j + 1) % (CB) == 0:
                    ins.then_inc(graph_unit, 1)
            for q in range(0, NCH, 2):
                dve.wait_ge(graph_T, q + 1)
                w = min(4, NB - 4 * q) * P
                dve.tensor_copy(graphT[:, q * NC:q * NC + w], ps_big[:, q % 4, 0:w]).then_inc(graph_out[0], 1)

            def add_x(k, par, g):
                n = k * NG + g
                dve.wait_ge(x_copied, n + 1)
                w = GS[g] * P
                x = xT[:, (par + g) % 2, 0:w]
                if g == 0:
                    wait(dve, hs_ready, k)
                    dve.tensor_copy(x_sum, x).then_inc(x_added, 1)
                else:
                    dve.wait_ge(x_added, n)
                    dve.tensor_tensor(x_sum[:, 0:w], x_sum[:, 0:w], x, ALU.add).then_inc(x_added, 1)

            def mean(k):
                dve.wait_ge(x_added, (k + 1) * NG)
                dve.tensor_reduce(hsT, x_sum.rearrange("p (j b) -> p b j", b=P), AX_X, ALU.add).then_inc(hs_ready, 1)

            def share(k):
                dve.wait_ge(hg_ready, k + 1)
                wait(dve, z_made, k * NG)
                dve.scalar_tensor_tensor(out=hg, in0=hg_ps, scalar=rcnt[:, bass.ds(k, 1)], in1=b1_row[:],
                                         op0=ALU.mult, op1=ALU.add).then_inc(hg_copied, 1)
                dve.wait_ge(hg_copied, k + 1)

            def add_z(k, par, g):
                n = k * NG + g
                w = GS[g] * P
                dve.wait_ge(g_ready, n + 1)
                dve.tensor_tensor(z[:, (par + g) % 2, 0:w].rearrange("p (j b) -> p j b", b=P),
                                  ps_g[:, (par + g) % 2, 0:w].rearrange("p (j b) -> p j b", b=P),
                                  hg.unsqueeze(1).to_broadcast([P, GS[g], P]), ALU.add).then_inc(z_made, 1)

            def weigh(k, par, g):
                n = k * NG + g
                dve.wait_ge(gate_made, n + 1)
                for j in range(GS[g]):
                    l = 4 * g + j
                    v = gate[:, (par + g) % 2, j * P:(j + 1) * P]
                    t = dve.scalar_tensor_tensor(out=v, in0=v, scalar=1.0, in1=w2_row[:], op0=ALU.mult, op1=ALU.mult,
                                                 accum_out=beta[:, l:l + 1])
                t.then_inc(beta_made, 1)
                dve.wait_ge(beta_made, n + 1)
                if g:
                    dve.wait_ge(sess_added, n)
                else:
                    wait(dve, sess_made, k)
                for j in range(GS[g]):
                    l = 4 * g + j
                    x = seq[:, par, l, :]
                    if g == 0:
                        t = dve.tensor_scalar(sess_sum[:, j, :], x, beta[:, l:l + 1], None, ALU.mult)
                    else:
                        t = dve.scalar_tensor_tensor(out=sess_sum[:, j, :], in0=x, scalar=beta[:, l:l + 1], in1=sess_sum[:, j, :],
                                                     op0=ALU.mult, op1=ALU.add)
                t.then_inc(sess_added, 1)

            def session(k):
                dve.wait_ge(sess_added, (k + 1) * NG)
                wait(dve, sel_ready, k)
                dve.tensor_reduce(sess, sess_sum.rearrange("p j d -> p d j"), AX_X, ALU.add).then_inc(sess_made, 1)
                dve.wait_ge(sess_made, k + 1)
                dve.scalar_tensor_tensor(out=sess_sq, in0=sess, scalar=1.0, in1=sess, op0=ALU.mult, op1=ALU.mult,
                                         accum_out=sess_n[:, 0:1]).then_inc(sess_ssq, 1)

            def select(k):
                dve.wait_ge(sess_nrm, k + 1)
                dve.tensor_scalar(sess_n[:, 2:3], sess_n[:, 1:2], EPS, None, ALU.max).then_inc(sel_chain, 1)
                dve.wait_ge(sel_chain, k * 2 + 1)
                dve.reciprocal(sess_n[:, 3:4], sess_n[:, 2:3]).then_inc(sel_chain, 1)
                dve.wait_ge(sel_chain, k * 2 + 2)
                dve.tensor_scalar(sel, sess, sess_n[:, 3:4], W_K, ALU.mult, ALU.mult).then_inc(sel_ready, 1)

            def selected(k):
                dve.wait_ge(selT_ready, k + 1)
                dve.tensor_copy(selT, selT_ps).then_inc(selT_copied, 1)

            def evacuate(k, kap, par, c):
                bank, before = score_slot(kap, par, c)
                if bank == 0:
                    dve.wait_ge(scored, k * NCH + c + 1)
                    u = c // 2
                    dve.wait_ge(stored[u % STAGES], (k * USES[u % STAGES] + u // STAGES) * 16 + 16)
                    dve.tensor_copy(stage[:, u % STAGES, c % 2 * NC:c % 2 * NC + width(c)], ps_s[:, 0, 0:width(c)])\
                        .then_inc(scores_out[0], 1)

            def lap(k, kap, par, has):
                takes, weighs, scores = has
                for g in range(NG):
                    if takes:
                        add_x(k, par, g)
                    if scores and g == 0:
                        select(k - 2)
                    if weighs:
                        if g == 0:
                            share(k - 1)
                        add_z(k - 1, 1 - par, g)
                        if g >= 1:
                            weigh(k - 1, 1 - par, g - 1)
                    if scores:
                        if g == 0:
                            selected(k - 2)
                        for c in CHUNKS[g]:
                            evacuate(k - 2, kap - 1, par, c)
                if takes:
                    mean(k)
                if weighs:
                    weigh(k - 1, 1 - par, NG - 1)
                    session(k - 1)

            dve.wait_ge(graph_out[1], NCH // 2)
            dve.memset(tick[:, 0:1], 0.0).then_inc(scores_out[0], 1)
            nc.disable_value_cache = True
            laps(lap)(dve)


_INS = ['r_items', 'r_inputs', 'r_alias_inputs', 'L0_rec_adj_row', 'L0_rec_adj_col', 'L0_rec_adj_val', 'L0_rec_E',
        'L0_rec_pos_emb', 'L0_rec_w1', 'L0_rec_w2', 'L0_rec_glu1_w', 'L0_rec_glu1_b', 'L0_rec_glu2_w']
_OUTS = [((1024, 12500), 'float32')]


def kernel(**inputs):
    import numpy as _np
    import concourse.bacc as _bacc
    from concourse import mybir as _mybir
    from concourse.bass_utils import run_bass_kernel_spmd as _run

    nc = _bacc.Bacc("TRN2", target_bir_lowering=False, num_devices=1)
    arrays, args = {}, []
    for name in _INS:
        a = _np.ascontiguousarray(inputs[name])
        arrays[f"in_{name}_dram"] = a
        args.append(nc.dram_tensor(f"in_{name}_dram", a.shape, _mybir.dt.from_np(a.dtype), kind="ExternalInput").ap())
    for i, (shape, dtype) in enumerate(_OUTS):
        dt = _mybir.dt.from_np(_np.dtype(dtype))
        args.append(nc.dram_tensor(f"out_{i}_dram", shape, dt, kind="ExternalOutput").ap())
    rec_kernel(nc, *args)
    r = _run(nc, [arrays], core_ids=[0])
    return r.results[0]["out_0_dram"]
```
